# Optimizing a Trainium2 kernel written in Bass

```python
import numpy as np
import jax
import jax.numpy as jnp

def _softmax(x, axis=-1):
    return jax.nn.softmax(x, axis=axis)

def _gelu(x):
    return jax.nn.gelu(x, approximate=True)

def _silu(x):
    return jax.nn.silu(x)

def _sigmoid(x):
    return jax.nn.sigmoid(x)

def _layernorm(x, axis=-1, eps=1e-05):
    m = jnp.mean(x, axis=axis, keepdims=True)
    v = jnp.var(x, axis=axis, keepdims=True)
    return (x - m) / jnp.sqrt(v + eps)

def _scatter_add(tgt, idx, src, axis=0):
    return tgt.at[idx].add(src)

def _segment_sum(src, seg, n):
    return jax.ops.segment_sum(src, seg, n)
kernel_name = 'mk_xattn_seq_d1_seqx_r4_e76003'

def setup_inputs(seed: int=0):
    np.random.seed(seed)
    _w = jnp.asarray

    def _rec_inputs():
        import jax
        import jax.numpy as jnp
        _rk = jax.random.key(seed)
        x = -0.0002928 + 1 * jax.random.normal(jax.random.fold_in(_rk, 1), (4, 1024, 256), jnp.float32)
        _lenS = 1024 - jax.random.randint(jax.random.fold_in(_rk, 7), (4,), 0, max(1, 1024 // 4) + 1, jnp.int32)
        _lenS2 = 64 - jax.random.randint(jax.random.fold_in(_rk, 8), (4,), 0, max(1, 64 // 4) + 1, jnp.int32)
        _ctx_1024P = jax.random.normal(jax.random.fold_in(_rk, 11), (4, 16, 256), jnp.float32)
        _ctx_1024c = jax.random.dirichlet(jax.random.fold_in(_rk, 511), 0.3 * jnp.ones((16,), jnp.float32), (4, 64))
        _ctx_1024t = jnp.einsum('bsk,bkd->bsd', _ctx_1024c, _ctx_1024P)
        _ctx_1024t = _ctx_1024t * jax.lax.rsqrt(jnp.mean(jnp.square(_ctx_1024t)) + 1e-12) * 0.953939
        ctx_1024 = -1.39393e-06 + 0.999914 * (_ctx_1024t + 0.3 * jax.random.normal(jax.random.fold_in(_rk, 611), (4, 64, 256), jnp.float32))
        _validS = jnp.arange(1024)[None, :] < _lenS[:, None]
        _validS2 = jnp.arange(64)[None, :] < _lenS2[:, None]
        _causal = jnp.tril(jnp.ones((1024, 1024), dtype=bool))
        mask_BxSxS2_ik1 = jnp.where(jnp.broadcast_to(_validS2[:, None, :], (4, 1024, 64)), 1, 0).astype(jnp.int32)
        return (x, ctx_1024, mask_BxSxS2_ik1)
    x, ctx_1024, mask_BxSxS2_ik1 = _rec_inputs()

    def _L0_xattn_setup():
        import jax, jax.numpy as jnp
        import numpy as np
        D_MODEL = 256
        NUM_HEADS = 16
        D_K = D_MODEL // NUM_HEADS
        LN_EPS = 1e-05

        def _split_heads(x):
            B, S, _ = x.shape
            return x.reshape(B, S, NUM_HEADS, D_K).transpose(0, 2, 1, 3)
        key = jax.random.key(seed)
        ks = jax.random.split(key, 16)
        B, SQ, SK = (2, 512, 512)
        s = 1.0 / np.sqrt(D_MODEL)
        inp = {'query': jax.random.normal(ks[0], (B, SQ, D_MODEL), jnp.float32), 'key': jax.random.normal(ks[1], (B, SK, D_MODEL), jnp.float32), 'value': jax.random.normal(ks[2], (B, SK, D_MODEL), jnp.float32), 'mask': jax.random.randint(ks[3], (B, SQ, SK), 0, 2, jnp.int32), 'w_q': jax.random.normal(ks[4], (D_MODEL, D_MODEL), jnp.float32) * s, 'b_q': jnp.zeros((D_MODEL,), jnp.float32), 'w_k': jax.random.normal(ks[5], (D_MODEL, D_MODEL), jnp.float32) * s, 'b_k': jnp.zeros((D_MODEL,), jnp.float32), 'w_v': jax.random.normal(ks[6], (D_MODEL, D_MODEL), jnp.float32) * s, 'b_v': jnp.zeros((D_MODEL,), jnp.float32), 'w_o': jax.random.normal(ks[7], (D_MODEL, D_MODEL), jnp.float32) * s, 'b_o': jnp.zeros((D_MODEL,), jnp.float32), 'ln_gamma': jnp.ones((D_MODEL,), jnp.float32), 'ln_beta': jnp.zeros((D_MODEL,), jnp.float32)}
        return inp
    _L0_xattn_all = _L0_xattn_setup()
    _L0_xattn_in = {k: v for k, v in _L0_xattn_all.items() if k in ('w_q', 'b_q', 'w_k', 'b_k', 'w_v', 'b_v', 'w_o', 'b_o', 'ln_gamma', 'ln_beta')}
    del _L0_xattn_all
    return {'x': x, 'ctx_1024': ctx_1024, 'mask_BxSxS2_ik1': mask_BxSxS2_ik1, 'L0_xattn_w_q': _L0_xattn_in['w_q'], 'L0_xattn_b_q': _L0_xattn_in['b_q'], 'L0_xattn_w_k': _L0_xattn_in['w_k'], 'L0_xattn_b_k': _L0_xattn_in['b_k'], 'L0_xattn_w_v': _L0_xattn_in['w_v'], 'L0_xattn_b_v': _L0_xattn_in['b_v'], 'L0_xattn_w_o': _L0_xattn_in['w_o'], 'L0_xattn_b_o': _L0_xattn_in['b_o'], 'L0_xattn_ln_gamma': _L0_xattn_in['ln_gamma'], 'L0_xattn_ln_beta': _L0_xattn_in['ln_beta']}

def reference(x, ctx_1024, mask_BxSxS2_ik1, L0_xattn_w_q, L0_xattn_b_q, L0_xattn_w_k, L0_xattn_b_k, L0_xattn_w_v, L0_xattn_b_v, L0_xattn_w_o, L0_xattn_b_o, L0_xattn_ln_gamma, L0_xattn_ln_beta):
    import jax
    import jax.numpy as jnp

    def _L0_xattn_ref(query, key, value, mask, w_q, b_q, w_k, b_k, w_v, b_v, w_o, b_o, ln_gamma, ln_beta):
        import jax, jax.numpy as jnp
        import numpy as np
        D_MODEL = 256
        NUM_HEADS = 16
        D_K = D_MODEL // NUM_HEADS
        LN_EPS = 1e-05

        def _split_heads(x):
            B, S, _ = x.shape
            return x.reshape(B, S, NUM_HEADS, D_K).transpose(0, 2, 1, 3)
        residual = query
        Q = _split_heads(jnp.einsum('bsd,ed->bse', query, w_q) + b_q)
        K = _split_heads(jnp.einsum('bsd,ed->bse', key, w_k) + b_k)
        V = _split_heads(jnp.einsum('bsd,ed->bse', value, w_v) + b_v)
        scores = jnp.einsum('bhqd,bhkd->bhqk', Q, K) / jnp.sqrt(jnp.float32(D_K))
        scores = jnp.where(mask[:, None, :, :] == 0, jnp.float32(-1000000000.0), scores)
        attn = jax.nn.softmax(scores, axis=-1)
        ctx = jnp.einsum('bhqk,bhkd->bhqd', attn, V)
        B, H, SQ, Dk = ctx.shape
        ctx = ctx.transpose(0, 2, 1, 3).reshape(B, SQ, D_MODEL)
        out = jnp.einsum('bsd,ed->bse', ctx, w_o) + b_o + residual
        mu = jnp.mean(out, axis=-1, keepdims=True)
        var = jnp.mean(jnp.square(out - mu), axis=-1, keepdims=True)
        out = (out - mu) * jax.lax.rsqrt(var + LN_EPS) * ln_gamma + ln_beta
        return out
    x = _L0_xattn_ref(x, ctx_1024, ctx_1024, mask_BxSxS2_ik1, L0_xattn_w_q, L0_xattn_b_q, L0_xattn_w_k, L0_xattn_b_k, L0_xattn_w_v, L0_xattn_b_v, L0_xattn_w_o, L0_xattn_b_o, L0_xattn_ln_gamma, L0_xattn_ln_beta)
    return x

_drawn_inputs = setup_inputs


def setup_inputs(seed=0):
    import zlib

    import numpy as np

    out = dict(_drawn_inputs(seed))
    spreads = {'L0_xattn_b_q': (0.0, 0.381),
     'L0_xattn_b_k': (0.0, 0.8),
     'L0_xattn_b_v': (0.0, 0.1),
     'L0_xattn_b_o': (0.0, 0.1),
     'L0_xattn_ln_gamma': (1.0, 0.2),
     'L0_xattn_ln_beta': (0.0, 0.1)}
    factors = {}
    for name, (base, spread) in spreads.items():
        noise = np.random.default_rng([zlib.crc32(name.encode()), seed]).standard_normal(out[name].shape)
        drawn = base * np.exp(spread * noise) if base else spread * noise
        out[name] = jnp.asarray(drawn.astype(out[name].dtype))
    for name, factor in factors.items():
        out[name] = (out[name] * factor).astype(out[name].dtype)
    return out
```

```python
from contextlib import ExitStack

import numpy as np

import concourse.bass as bass
from concourse import mybir

F32 = mybir.dt.float32
F32R = mybir.dt.float32r
I32 = mybir.dt.int32
ALU = mybir.AluOpType
ACT = mybir.ActivationFunctionType
AX_X = mybir.AxisListType.X

P = 128
BATCHES, QUERIES, KEYS, D = 4, 1024, 64, 256
HEADS = 16
DK = D // HEADS
CHUNK = 512
TILES = CHUNK // P
PER_BATCH = QUERIES // CHUNK
CHUNKS = BATCHES * PER_BATCH
PAIRS = HEADS // 2
PC = D // P
QB = 8
QN = CHUNK // QB
SCALE = float(DK) ** -0.5
BIG = 2.0 ** 100
EPS = 1e-5
NQ = 3
NP_ = 3

IDENT, ID64, BLOCK, ONES = 0, P, P + KEYS, P + KEYS + 4
CONSTS = ONES + 2 * 32


def build(nc, xT, x, maskT, ctxT, wq, wk, wv, wo, bias_cols, bias_rows, consts, out):
    with ExitStack() as ctx:
        def sb(name, shape, dt=F32):
            return ctx.enter_context(nc.sbuf_tensor(name, shape, dt))

        def bank(name, n=1):
            return ctx.enter_context(nc.psum_tensor(name, [P, n, 512], F32))

        def sem(name):
            return ctx.enter_context(nc.semaphore(name))

        con = sb("con", [P, CONSTS])
        bcol = sb("bcol", [P, 4])
        brow = sb("brow", [P, 4, D])
        ctx_t = sb("ctx_t", [P, PC, BATCHES, 2, KEYS])
        wq_sb = sb("wq_sb", [P, PC, D])
        wk_sb = sb("wk_sb", [P, PC, D])
        wv_sb = sb("wv_sb", [P, PC, D])
        wo_sb = sb("wo_sb", [P, PC, D])
        wq_h = sb("wq_h", [P, PC, D], F32R)
        wq_l = sb("wq_l", [P, PC, D], F32R)
        kt = sb("kt", [P, 2, BATCHES, KEYS])
        k_h = sb("k_h", [P, 2, BATCHES, KEYS], F32R)
        k_l = sb("k_l", [P, 2, BATCHES, KEYS], F32R)
        keys_mask = sb("keys_mask", [P, 2, 2, 2, 256], F32R)
        keys_low = sb("keys_low", [P, 2, 2, 2, 256], F32R)
        keys_max = sb("keys_max", [P, 2, 2, 2, 256], F32R)
        v_bd = sb("v_bd", [P, BATCHES, PAIRS, 32])
        xt_sb = sb("xt_sb", [P, 2, PC, CHUNK])
        xt_h = sb("xt_h", [P, 2, PC, CHUNK], F32R)
        xt_l = sb("xt_l", [P, 2, PC, CHUNK], F32R)
        m_sb = sb("m_sb", [KEYS, 2, CHUNK], I32)
        q_high = sb("q_high", [P, NQ, 2, 2, CHUNK], F32R)
        q_low = sb("q_low", [P, NQ, 2, 2, CHUNK], F32R)
        nmax = sb("nmax", [P, 2, TILES, HEADS])
        probs = sb("probs", [P, NP_, CHUNK])
        cx = sb("cx", [P, 2, 2, CHUNK])
        den_sb = sb("den_sb", [P, 2, CHUNK])
        den_t = sb("den_t", [P, 2, QN])
        rec_t = sb("rec_t", [P, 2, QN])
        rec = sb("rec", [P, 2, 2, CHUNK])
        cn = sb("cn", [P, 2, 2, CHUNK])
        x_sb = sb("x_sb", [P, 3, TILES, D])
        xb = sb("xb", [P, 3, TILES, D])
        res = sb("res", [P, 2, TILES, D])
        stat = sb("stat", [P, 2, TILES, 6])
        mv = sb("mv", [P, 2, TILES, 2])
        veps = sb("veps", [P, 2, TILES])
        rstd = sb("rstd", [P, 2, TILES])
        nmean = sb("nmean", [P, 2, TILES])
        shift = sb("shift", [P, 2, TILES])
        half_neg = sb("half_neg", [P, TILES])
        y = sb("y", [P, 2, TILES, D])

        rec_dram = nc.dram_tensor("rec_dram", (2, P, QN), F32, kind="Internal").ap()

        ps_max = bank("ps_max", 2)
        ps_s = bank("ps_s", 2)
        ps_c = bank("ps_c")
        ps_d = bank("ps_d")
        ps_q = bank("ps_q")
        ps_o = bank("ps_o")

        in_con, in_ctx, in_wk, in_wq, in_wv, in_wo, in_rows = (sem(n) for n in (
            "in_con", "in_ctx", "in_wk", "in_wq", "in_wv", "in_wo", "in_rows"))
        in_xt = [sem(f"in_xt{i}") for i in range(2)]
        in_mask = [sem(f"in_mask{i}") for i in range(2)]
        in_x = [sem(f"in_x{i}") for i in range(3)]
        k_done, v_done = sem("k_done"), sem("v_done")
        q_done, max_done, turn_done = sem("q_done"), sem("max_done"), sem("turn_done")
        s_done, pv_done, o_done = sem("s_done"), sem("pv_done"), sem("o_done")
        wqh_done, kh_done, kfix_done, kmax_done = sem("wqh_done"), sem("kh_done"), sem("kfix_done"), sem("kmax_done")
        xh_done, h_done, e_done, neg_done = sem("xh_done"), sem("h_done"), sem("e_done"), sem("neg_done")
        cx_done, den_done, y_done = sem("cx_done"), sem("den_done"), sem("y_done")
        wql_done, kt_done, kl_done, kblk_done, vbd_done = (sem(n) for n in (
            "wql_done", "kt_done", "kl_done", "kblk_done", "vbd_done"))
        xl_done, mask_done, l_done, nm_done = sem("xl_done"), sem("mask_done"), sem("l_done"), sem("nm_done")
        rec_done, cn_done, res_done, bn_done, mv_done = (sem(n) for n in (
            "rec_done", "cn_done", "res_done", "bn_done", "mv_done"))
        fill_done, xb_done, ln_done, gam_done, bet_done = (sem(n) for n in (
            "fill_done", "xb_done", "ln_done", "gam_done", "bet_done"))
        den_in = [sem(f"den_in{i}") for i in range(2)]
        rec_out = [sem(f"rec_out{i}") for i in range(2)]
        rec_in = [sem(f"rec_in{i}") for i in range(2)]
        stored = [sem(f"stored{i}") for i in range(2)]

        def region(p):
            return p // 4, (p // 2) % 2, p % 2

        def rows(half):
            return slice(64 * half, 64 * half + 64)

        REC_DMAS, DEN_DMAS = 2, 4

        block = ctx.enter_context(nc.Block())

        @block.sync
        def _(sp):
            def load_xt(c):
                if c >= 2:
                    sp.wait_ge(xl_done, c - 1)
                    sp.wait_ge(xh_done, c - 1)
                sp.dma_start(xt_sb[:, c % 2], xT[c]).then_inc(in_xt[c % 2], 16)

            def load_mask(c):
                if c >= 2:
                    sp.wait_ge(mask_done, 2 * (c - 1))
                sp.dma_start(m_sb[:, c % 2], maskT[c]).then_inc(in_mask[c % 2], 16)

            def load_x(c):
                if c >= 3:
                    sp.wait_ge(xb_done, c - 2)
                sp.dma_start(x_sb[:, c % 3], x[c]).then_inc(in_x[c % 3], 16)

            def spread_denominators(c):
                sp.wait_ge(den_done, c + 1)
                if c >= 2:
                    sp.wait_ge(rec_done, c - 1)
                for quad in range(4):
                    sp.dma_start(den_t[32 * quad:32 * quad + 32, c % 2],
                                 den_sb[32 * quad:32 * quad + 4, c % 2].rearrange("r (b n) -> r b n", b=QB)
                                 ).then_inc(den_in[c % 2], 16)

            def broadcast_reciprocals(c):
                sp.wait_ge(rec_done, c + 1)
                if c >= 2:
                    sp.wait_ge(cn_done, 2 * (c - 1))
                sp.dma_start(rec_dram[c % 2], rec_t[:, c % 2]).then_inc(rec_out[c % 2], 16)
                sp.wait_ge(rec_out[c % 2], 16 * (c // 2 + 1))
                for j in range(2):
                    sp.dma_start(rec[:, c % 2, j],
                                 rec_dram[c % 2].rearrange("(g j b) n -> g j (b n)", j=2, b=QB)[:, j]
                                 .unsqueeze(1).to_broadcast([8, DK, CHUNK])).then_inc(rec_in[c % 2], 16)

            def store(c):
                sp.wait_ge(bet_done, c + 1)
                sp.dma_start(out[c], y[:, c % 2]).then_inc(stored[c % 2], 16)

            sp.dma_start(ctx_t[:], ctxT).then_inc(in_ctx, 16)
            sp.dma_start(wk_sb[:], wk).then_inc(in_wk, 16)
            load_xt(0)
            sp.dma_start(wq_sb[:], wq).then_inc(in_wq, 16)
            sp.dma_start(con[:], consts).then_inc(in_con, 16)
            sp.dma_start(bcol[:], bias_cols).then_inc(in_con, 16)
            load_mask(0)
            sp.dma_start(wv_sb[:], wv).then_inc(in_wv, 16)
            sp.dma_start(brow[:], bias_rows.to_broadcast([P, 4, D])).then_inc(in_rows, 16)
            load_xt(1)
            load_mask(1)
            load_x(0)
            sp.dma_start(wo_sb[:], wo).then_inc(in_wo, 16)
            for step in range(CHUNKS + 3):
                if step + 2 < CHUNKS:
                    load_xt(step + 2)
                    load_mask(step + 2)
                if step + 1 < CHUNKS:
                    load_x(step + 1)
                if 0 <= step - 2 < CHUNKS:
                    spread_denominators(step - 2)
                if 0 <= step - 4 < CHUNKS:
                    store(step - 4)
                if 0 <= step - 2 < CHUNKS:
                    broadcast_reciprocals(step - 2)
            store(CHUNKS - 1)
            for c in (CHUNKS - 2, CHUNKS - 1):
                sp.wait_ge(stored[c % 2], 16 * (c // 2 + 1))

        @block.tensor
        def _(pe):
            def project_keys():
                pe.wait_ge(in_ctx, 16)
                pe.wait_ge(in_wk, 16)
                for j in range(2):
                    for d in range(PC):
                        mm = pe.matmul(ps_max[:, j, 0:256], wk_sb[:, d, j * P:(j + 1) * P],
                                       ctx_t[:, d, :, 0, :], start=d == 0, stop=d == PC - 1)
                mm.then_inc(k_done, 1)

            def project_values():
                pe.wait_ge(in_wv, 16)
                for b in range(BATCHES):
                    for d in range(PC):
                        mm = pe.matmul(ps_s[:, b // 2, (b % 2) * 256:(b % 2) * 256 + 256],
                                       ctx_t[:, d, b], wv_sb[:, d], start=d == 0, stop=d == PC - 1)
                mm.then_inc(v_done, 1)

            def project_queries(c, j):
                pe.wait_ge(xh_done, c + 1)
                pe.wait_ge(xl_done, c + 1)
                n = 2 * c + j
                if n == 0:
                    pe.wait_ge(wqh_done, 1)
                    pe.wait_ge(wql_done, 1)
                else:
                    pe.wait_ge(l_done, 2 * n)
                for d in range(PC):
                    for w, a in ((wq_h, xt_h), (wq_l, xt_h), (wq_h, xt_l)):
                        mm = pe.matmul(ps_q[:, 0], w[:, d, j * P:(j + 1) * P], a[:, c % 2, d],
                                       start=d == 0 and w is wq_h and a is xt_h,
                                       stop=d == PC - 1 and a is xt_l)
                mm.then_inc(q_done, 1)

            def max_scores(c, t):
                n = TILES * c + t
                s = (c // PER_BATCH) % 2
                if t == 0:
                    pe.wait_ge(h_done, 4 * (c + 1))
                    pe.wait_ge(mask_done, 2 * (c + 1))
                    pe.wait_ge(kblk_done, 4 * (c // PER_BATCH + 1))
                    pe.wait_ge(kfix_done, 2)
                    if n == 0:
                        pe.wait_ge(kt_done, 2)
                if n:
                    pe.wait_ge(nm_done, n)
                for half in range(2):
                    for j in range(2):
                        g = 2 * half + j
                        mm = pe.matmul(ps_max[:, g // 2, (g % 2) * 256:(g % 2) * 256 + 256],
                                       q_high[:, c % NQ, half, j, t * P:(t + 1) * P],
                                       keys_mask[:, s, half, j], start=True, stop=True)
                mm.then_inc(max_done, 1)

            def turn_max(c):
                pe.wait_ge(nm_done, TILES * (c + 1))
                if c >= 3:
                    pe.wait_ge(res_done, 2 * (c - 2))
                if c == 0:
                    pe.wait_ge(in_con, 32)
                for t in range(TILES):
                    mm = pe.transpose(ps_o[0:HEADS, 0, t * P:(t + 1) * P], nmax[:, c % 2, t],
                                      con[:, IDENT:IDENT + P])
                mm.then_inc(turn_done, 1)

            def scores(c, p):
                k = PAIRS * c + p
                j, half, pp = region(p)
                s = (c // PER_BATCH) % 2
                if k == 0:
                    pe.wait_ge(vbd_done, 2 * BATCHES)
                if k >= 2:
                    pe.wait_ge(e_done, k - 1)
                if p == 0:
                    pe.wait_ge(kmax_done, 2 * (c // PER_BATCH + 1))
                    pe.wait_ge(l_done, 4 * (c + 1))
                lo, hi = pp * P, pp * P + P
                pe.matmul(ps_s[:, k % 2], keys_mask[:, s, half, j, lo:hi], q_high[:, c % NQ, half, j],
                          start=True, stop=False)
                pe.matmul(ps_s[:, k % 2], keys_low[:, s, half, j, lo:hi], q_high[:, c % NQ, half, j],
                          start=False, stop=False)
                if p == 0:
                    pe.wait_ge(neg_done, 2 * (c + 1))
                pe.matmul(ps_s[:, k % 2], keys_max[:, s, half, j, lo:hi], q_low[:, c % NQ, half, j],
                          start=False, stop=True).then_inc(s_done, 1)

            def values(k):
                c, p = divmod(k, PAIRS)
                b = c // PER_BATCH
                j, quad = p // 4, p % 4
                pe.wait_ge(e_done, k + 1)
                if quad == 0 and 2 * c + j >= 1:
                    pe.wait_ge(cx_done, 2 * c + j)
                pe.matmul(ps_c[32 * quad:32 * quad + 32, 0], v_bd[:, b, p], probs[:, k % NP_],
                          start=True, stop=True)
                if p == 0 and c >= 1:
                    pe.wait_ge(den_done, c)
                pe.matmul(ps_d[32 * quad:32 * quad + 32, 0], con[:, ONES + 32 * j:ONES + 32 * j + 32],
                          probs[:, k % NP_], start=j == 0, stop=j == 1,
                          skip_group_check=True).then_inc(pv_done, 1)

            def output(c, i):
                if c == 0 and i == 0:
                    pe.wait_ge(in_wo, 16)
                pe.wait_ge(cn_done, 2 * (c + 1))
                if i == 0:
                    pe.wait_ge(res_done, 2 * c) if c else None
                    pe.wait_ge(neg_done, 2 * min(c + 3, CHUNKS))
                else:
                    pe.wait_ge(res_done, 2 * c + 1)
                for t in range(2):
                    for j in range(PC):
                        mm = pe.matmul(ps_o[:, 0, t * 256:t * 256 + 256],
                                       cn[:, c % 2, j, (2 * i + t) * P:(2 * i + t + 1) * P], wo_sb[:, j],
                                       start=j == 0, stop=j == PC - 1)
                mm.then_inc(o_done, 1)

            project_keys()
            project_queries(0, 0)
            project_queries(0, 1)
            project_values()
            max_scores(0, 0)
            max_scores(0, 1)
            for step in range(CHUNKS + 2):
                front, back, last = step, step - 1, step - 2
                for slot in range(PAIRS):
                    k = PAIRS * back + slot
                    if 0 <= back < CHUNKS:
                        scores(back, slot)
                    if 0 <= k - 1 < PAIRS * CHUNKS:
                        values(k - 1)
                    if slot in (0, 3) and front + 1 < CHUNKS:
                        project_queries(front + 1, slot // 3)
                    if slot in (0, 2) and front < CHUNKS:
                        max_scores(front, 2 + slot // 2)
                    if slot == 4 and front < CHUNKS:
                        turn_max(front)
                    if slot in (5, 7) and front + 1 < CHUNKS:
                        max_scores(front + 1, (slot - 5) // 2)
                    if slot in (6, 7) and 0 <= last < CHUNKS:
                        output(last, slot - 6)

        @block.scalar
        def _(act):
            def high_x(c):
                act.wait_ge(in_xt[c % 2], 16 * (c // 2 + 1))
                if c >= 2:
                    act.wait_ge(q_done, 2 * (c - 1))
                act.activation(xt_h[:, c % 2], xt_sb[:, c % 2], ACT.Copy).then_inc(xh_done, 1)

            def high_queries(c, j):
                act.wait_ge(q_done, 2 * c + j + 1)
                if c >= NQ:
                    act.wait_ge(s_done, PAIRS * (c - NQ + 1))
                for half in range(2):
                    act.activation(q_high[rows(half), c % NQ, half, j], ps_q[rows(half), 0], ACT.Identity,
                                   bias=bcol[rows(half), j:j + 1]).then_inc(h_done, 1)

            def fixed_rows():
                act.wait_ge(in_con, 32)
                act.wait_ge(fill_done, 1)
                for half in range(2):
                    other = rows(1 - half)
                    id64 = con[other, ID64:ID64 + KEYS]
                    for dst, src in (
                        (keys_mask, id64.unsqueeze(1).to_broadcast([64, 8, KEYS])),
                        (keys_max, id64[:, 8 * half:8 * half + 8].unsqueeze(2).to_broadcast([64, 8, KEYS])),
                    ):
                        for s in range(2):
                            fixed = act.activation(dst[other, s, half].rearrange("p j (h k) -> p (j h) k", k=KEYS),
                                                   src, ACT.Copy)
                    fixed.then_inc(kfix_done, 1)

            def max_blocks(b):
                act.wait_ge(kblk_done, 4 * b + 4)
                if b >= 2:
                    act.wait_ge(s_done, PAIRS * PER_BATCH * (b - 1))
                for half in range(2):
                    act.activation(keys_max[rows(half), b % 2, half], keys_mask[rows(half), b % 2, half].bitcast(F32),
                                   ACT.Copy).then_inc(kmax_done, 1)

            def exponentials(k):
                act.wait_ge(s_done, k + 1)
                if k >= NP_:
                    act.wait_ge(pv_done, k - NP_ + 1)
                act.activation(probs[:, k % NP_], ps_s[:, k % 2], ACT.Exp).then_inc(e_done, 1)

            def negative_max(c):
                act.wait_ge(turn_done, c + 1)
                if c == 0:
                    act.wait_ge(fill_done, 2)
                if c >= NQ:
                    act.wait_ge(s_done, PAIRS * (c - NQ + 1))
                for half in range(2):
                    o = 64 * (1 - half)
                    act.activation(q_low[o:o + HEADS, c % NQ, half],
                                   ps_o[0:HEADS, 0].unsqueeze(1).to_broadcast([HEADS, 2, CHUNK]),
                                   ACT.Copy).then_inc(neg_done, 1)

            def context_out(c, j):
                act.wait_ge(pv_done, PAIRS * c + 4 * j + 4)
                if c >= 2:
                    act.wait_ge(cn_done, 2 * (c - 1))
                act.activation(cx[:, c % 2, j], ps_c[:, 0], ACT.Copy).then_inc(cx_done, 1)

            def denominators_out(c):
                act.wait_ge(pv_done, PAIRS * (c + 1))
                if c >= 2:
                    act.wait_ge(den_in[c % 2], 16 * DEN_DMAS * (c // 2))
                act.activation(den_sb[:, c % 2], ps_d[:, 0], ACT.Copy).then_inc(den_done, 1)

            def normalised(c, t):
                act.wait_ge(ln_done, 4 * (c + 1))
                if c >= 2:
                    act.wait_ge(stored[c % 2], 16 * (c // 2))
                act.activation(y[:, c % 2, t], res[:, c % 2, t], ACT.Identity, bias=shift[:, c % 2, t:t + 1],
                               scale=rstd[:, c % 2, t:t + 1]).then_inc(y_done, 1)

            act.wait_ge(in_wq, 16)
            act.activation(wq_h[:], wq_sb[:], ACT.Copy).then_inc(wqh_done, 1)
            high_x(0)
            act.wait_ge(kt_done, 2)
            act.activation(k_h[:], kt[:], ACT.Copy).then_inc(kh_done, 1)
            fixed_rows()
            high_queries(0, 0)
            high_queries(0, 1)
            max_blocks(0)
            high_x(1)
            for step in range(CHUNKS + 3):
                front, back, last, norm = step, step - 1, step - 2, step - 3
                for slot in range(PAIRS):
                    if 0 <= back < CHUNKS:
                        exponentials(PAIRS * back + slot)
                    if slot == 0 and 0 <= last < CHUNKS:
                        context_out(last, 1)
                        denominators_out(last)
                    if slot == 4 and 0 <= back < CHUNKS:
                        context_out(back, 0)
                    if slot in (1, 4) and front + 1 < CHUNKS:
                        high_queries(front + 1, slot // 4)
                    if slot == 2 and front + 2 < CHUNKS:
                        high_x(front + 2)
                    if slot == 3 and front % PER_BATCH == PER_BATCH - 1 and front // PER_BATCH + 1 < BATCHES:
                        max_blocks(front // PER_BATCH + 1)
                    if slot == 5 and front < CHUNKS:
                        negative_max(front)
                    if slot in (2, 3, 6, 7) and 0 <= norm < CHUNKS:
                        normalised(norm, (2, 3, 6, 7).index(slot))

        @block.vector
        def _(dve):
            def low_x(c):
                dve.wait_ge(xh_done, c + 1)
                if c >= 2:
                    dve.wait_ge(q_done, 2 * (c - 1))
                dve.tensor_tensor(xt_l[:, c % 2], xt_sb[:, c % 2], xt_h[:, c % 2].bitcast(F32),
                                  ALU.subtract).then_inc(xl_done, 1)

            def mask_rows(c):
                dve.wait_ge(in_mask[c % 2], 16 * (c // 2 + 1))
                if c >= NQ:
                    dve.wait_ge(s_done, PAIRS * (c - NQ + 1))
                for half in range(2):
                    dve.tensor_scalar(q_high[rows(1 - half), c % NQ, half],
                                      m_sb[:, c % 2].unsqueeze(1).to_broadcast([KEYS, 2, CHUNK]),
                                      0.0, -BIG, ALU.is_equal, ALU.mult).then_inc(mask_done, 1)

            def low_queries(c, j):
                if c >= NQ:
                    dve.wait_ge(s_done, PAIRS * (c - NQ + 1))
                for half in range(2):
                    dve.wait_ge(h_done, 4 * c + 2 * j + half + 1)
                    dve.scalar_tensor_tensor(q_low[rows(half), c % NQ, half, j], ps_q[rows(half), 0],
                                             bcol[rows(half), j:j + 1],
                                             q_high[rows(half), c % NQ, half, j].bitcast(F32),
                                             ALU.add, ALU.subtract).then_inc(l_done, 1)

            def maxima(c, t):
                dve.wait_ge(max_done, TILES * c + t + 1)
                if c >= 2:
                    dve.wait_ge(turn_done, c - 1)
                dve.tensor_reduce(nmax[:, c % 2, t], ps_max[:].rearrange("p a (h k) -> p (a h) k", k=KEYS),
                                  AX_X, ALU.max, negate=True).then_inc(nm_done, 1)

            def key_blocks(b):
                if b >= 2:
                    dve.wait_ge(s_done, PAIRS * PER_BATCH * (b - 1))
                for half in range(2):
                    r = rows(half)
                    pick = con[r, BLOCK:BLOCK + 4].unsqueeze(2).to_broadcast([64, 4, KEYS])
                    for dst, src in ((keys_mask, k_h), (keys_low, k_l)):
                        for j in range(2):
                            blk = dve.tensor_tensor(dst[r, b % 2, half, j].rearrange("p (h k) -> p h k", k=KEYS),
                                                    src[r, j, b].bitcast(F32).unsqueeze(1).to_broadcast([64, 4, KEYS]),
                                                    pick, ALU.mult)
                        blk.then_inc(kblk_done, 1)

            def reciprocals(c):
                dve.wait_ge(den_in[c % 2], 16 * DEN_DMAS * (c // 2 + 1))
                if c >= 2:
                    dve.wait_ge(rec_in[c % 2], 16 * REC_DMAS * (c // 2))
                dve.reciprocal(rec_t[:, c % 2], den_t[:, c % 2]).then_inc(rec_done, 1)

            def divide(c):
                dve.wait_ge(rec_in[c % 2], 16 * REC_DMAS * (c // 2 + 1))
                dve.wait_ge(cx_done, 2 * (c + 1))
                if c >= 2:
                    dve.wait_ge(o_done, 2 * (c - 1))
                for j in range(2):
                    dve.tensor_tensor(cn[:, c % 2, j], cx[:, c % 2, j], rec[:, c % 2, j],
                                      ALU.mult).then_inc(cn_done, 1)

            def residual(c, i):
                dve.wait_ge(o_done, 2 * c + i + 1)
                dve.wait_ge(xb_done, c + 1)
                if c >= 2:
                    dve.wait_ge(y_done, TILES * (c - 1))
                two = slice(2 * i, 2 * i + 2)
                dve.tensor_tensor(res[:, c % 2, two], ps_o[:, 0].rearrange("p (t d) -> p t d", t=2),
                                  xb[:, c % 3, two], ALU.add).then_inc(res_done, 1)

            def moments(c, i):
                n = 2 * c + i + 1
                dve.wait_ge(res_done, n)
                if c >= 2:
                    dve.wait_ge(ln_done, 4 * (c - 1))
                for t in (2 * i, 2 * i + 1):
                    dve.bn_stats(stat[:, c % 2, t], res[:, c % 2, t]).then_inc(bn_done, 1)
                dve.wait_ge(bn_done, 2 * n)
                for t in (2 * i, 2 * i + 1):
                    dve.bn_aggr(mv[:, c % 2, t], stat[:, c % 2, t]).then_inc(mv_done, 1)

            dve.wait_ge(k_done, 1)
            dve.wait_ge(in_con, 32)
            for j in range(2):
                dve.tensor_scalar(kt[:, j], ps_max[:, j, 0:256].rearrange("p (b k) -> p b k", k=KEYS),
                                  bcol[:, 2 + j:3 + j], SCALE, ALU.add, ALU.mult).then_inc(kt_done, 1)
            dve.wait_ge(wqh_done, 1)
            dve.tensor_tensor(wq_l[:], wq_sb[:], wq_h[:].bitcast(F32), ALU.subtract).then_inc(wql_done, 1)
            low_x(0)
            dve.wait_ge(kt_done, 2)
            dve.wait_ge(kh_done, 1)
            dve.tensor_tensor(k_l[:], kt[:], k_h[:].bitcast(F32), ALU.subtract).then_inc(kl_done, 1)
            mask_rows(0)
            dve.wait_ge(kl_done, 1)
            dve.wait_ge(fill_done, 1)
            key_blocks(0)
            dve.wait_ge(fill_done, 3)
            low_queries(0, 0)
            low_queries(0, 1)
            dve.wait_ge(v_done, 1)
            dve.wait_ge(in_rows, 16)
            for b in range(BATCHES):
                for h in range(2):
                    r = rows(h)
                    dve.tensor_tensor(
                        v_bd[r, b, :, 16 * h:16 * h + 16],
                        ps_s[r, b // 2, (b % 2) * 256:(b % 2) * 256 + 256].rearrange(
                            "k (p e) -> k p e", e=32)[:, :, 16 * h:16 * h + 16],
                        brow[r, 0].rearrange("k (p e) -> k p e", e=32)[:, :, 16 * h:16 * h + 16],
                        ALU.add).then_inc(vbd_done, 1)
            maxima(0, 0)
            maxima(0, 1)
            low_x(1)
            for step in range(CHUNKS + 3):
                front, last, norm = step, step - 2, step - 3
                for slot in range(PAIRS):
                    if slot == 0 and 0 <= norm < CHUNKS:
                        residual(norm, 1)
                        moments(norm, 1)
                    if slot == 1 and front + 1 < CHUNKS:
                        low_queries(front + 1, 0)
                    if slot in (0, 2) and front < CHUNKS:
                        maxima(front, 2 + slot // 2)
                    if slot == 2 and front % PER_BATCH == PER_BATCH - 1 and front // PER_BATCH + 1 < BATCHES:
                        key_blocks(front // PER_BATCH + 1)
                    if slot == 3 and front + 1 < CHUNKS:
                        mask_rows(front + 1)
                    if slot == 4 and 0 <= last < CHUNKS:
                        reciprocals(last)
                    if slot == 4 and front + 1 < CHUNKS:
                        low_queries(front + 1, 1)
                    if slot == 5 and front + 2 < CHUNKS:
                        low_x(front + 2)
                    if slot == 5 and front + 1 < CHUNKS:
                        maxima(front + 1, 0)
                    if slot == 6 and 0 <= last < CHUNKS:
                        divide(last)
                    if slot == 7 and 0 <= last < CHUNKS:
                        residual(last, 0)
                    if slot == 7 and front + 1 < CHUNKS:
                        maxima(front + 1, 1)
                    if slot == 7 and 0 <= last < CHUNKS:
                        moments(last, 0)

        @block.gpsimd
        def _(pool):
            def with_bias(c):
                pool.wait_ge(in_x[c % 3], 16 * (c // 3 + 1))
                if c >= 3:
                    pool.wait_ge(res_done, 2 * (c - 2))
                pool.tensor_tensor(xb[:, c % 3], x_sb[:, c % 3],
                                   brow[:, 1].unsqueeze(1).to_broadcast([P, TILES, D]), ALU.add).then_inc(xb_done, 1)

            def deviations(c):
                i = c % 2
                pool.wait_ge(mv_done, TILES * (c + 1))
                if c >= 2:
                    pool.wait_ge(y_done, TILES * (c - 1))
                pool.tensor_scalar(veps[:, i], mv[:, i, :, 1], EPS, 1.0, ALU.add, ALU.mult).then_inc(ln_done, 1)
                pool.tensor_scalar(nmean[:, i], mv[:, i, :, 0], -1.0, 0.0, ALU.mult, ALU.add).then_inc(ln_done, 1)
                pool.wait_ge(ln_done, 4 * c + 2)
                pool.tensor_tensor(rstd[:, i], veps[:, i], half_neg[:], ALU.pow).then_inc(ln_done, 1)
                pool.wait_ge(ln_done, 4 * c + 3)
                pool.tensor_tensor(shift[:, i], nmean[:, i], rstd[:, i], ALU.mult).then_inc(ln_done, 1)

            def affine(c):
                i = c % 2
                pool.wait_ge(y_done, TILES * (c + 1))
                pool.tensor_tensor(y[:, i], y[:, i], brow[:, 2].unsqueeze(1).to_broadcast([P, TILES, D]),
                                   ALU.mult).then_inc(gam_done, 1)
                pool.wait_ge(gam_done, c + 1)
                pool.tensor_tensor(y[:, i], y[:, i], brow[:, 3].unsqueeze(1).to_broadcast([P, TILES, D]),
                                   ALU.add).then_inc(bet_done, 1)

            pool.memset(keys_low[:].bitcast(F32), 0.0).then_inc(fill_done, 1)
            pool.memset(q_low[:].bitcast(F32), 0.0).then_inc(fill_done, 1)
            pool.memset(v_bd[:], 0.0).then_inc(fill_done, 1)
            pool.memset(half_neg[:], -0.5).then_inc(fill_done, 1)
            pool.wait_ge(fill_done, 4)
            pool.wait_ge(in_rows, 16)
            for step in range(CHUNKS + 3):
                if 0 <= step - 3 < CHUNKS:
                    deviations(step - 3)
                if 0 <= step - 1 < CHUNKS:
                    with_bias(step - 1)
                if 0 <= step - 3 < CHUNKS:
                    affine(step - 3)


def kernel(x, ctx_1024, mask_BxSxS2_ik1, L0_xattn_w_q, L0_xattn_b_q, L0_xattn_w_k, L0_xattn_b_k, L0_xattn_w_v,
           L0_xattn_b_v, L0_xattn_w_o, L0_xattn_b_o, L0_xattn_ln_gamma, L0_xattn_ln_beta):
    import concourse.bacc as bacc
    from concourse.bass_utils import run_bass_kernel_spmd

    x, ctx, mask = (np.asarray(a) for a in (x, ctx_1024, mask_BxSxS2_ik1))

    def weight(w):
        return np.ascontiguousarray(np.asarray(w).T.reshape(PC, P, D).transpose(1, 0, 2))

    chunks = x.reshape(CHUNKS, CHUNK, D)
    consts = np.zeros((P, CONSTS), np.float32)
    row = np.arange(P)
    consts[row, IDENT + row] = 1
    consts[row, ID64 + row % 64] = 1
    consts[row, BLOCK + row % 64 // DK] = 1
    for j in range(2):
        consts[row, ONES + 32 * j + 2 * (row // 64) + j] = 1
    arrays = {
        "xT": np.ascontiguousarray(chunks.transpose(0, 2, 1).reshape(CHUNKS, PC, P, CHUNK).transpose(0, 2, 1, 3)),
        "x": np.ascontiguousarray(chunks.reshape(CHUNKS, TILES, P, D).transpose(0, 2, 1, 3)),
        "maskT": np.ascontiguousarray(mask.reshape(CHUNKS, CHUNK, KEYS).transpose(0, 2, 1)),
        "ctxT": np.ascontiguousarray(np.broadcast_to(
            ctx.transpose(2, 0, 1).reshape(PC, P, BATCHES, 1, KEYS), (PC, P, BATCHES, 2, KEYS)
        ).transpose(1, 0, 2, 3, 4)),
        "wq": weight(L0_xattn_w_q), "wk": weight(L0_xattn_w_k),
        "wv": weight(L0_xattn_w_v), "wo": weight(L0_xattn_w_o),
        "bias_cols": np.ascontiguousarray(np.concatenate(
            [np.asarray(b).reshape(PC, P).T for b in (L0_xattn_b_q, L0_xattn_b_k)], axis=1)),
        "bias_rows": np.stack([np.asarray(b) for b in (
            L0_xattn_b_v, L0_xattn_b_o, L0_xattn_ln_gamma, L0_xattn_ln_beta)])[None],
        "consts": consts,
    }
    nc = bacc.Bacc("TRN2", target_bir_lowering=False, num_devices=1)
    args = [nc.dram_tensor(n, a.shape, mybir.dt.from_np(a.dtype), kind="ExternalInput").ap()
            for n, a in arrays.items()]
    out = nc.dram_tensor("out", (CHUNKS, P, TILES, D), F32, kind="ExternalOutput").ap()
    build(nc, *args, out)
    r = run_bass_kernel_spmd(nc, [arrays], core_ids=[0])
    return r.results[0]["out"].transpose(0, 2, 1, 3).reshape(BATCHES, QUERIES, D)
```

```python
from contextlib import ExitStack

import numpy as np

import concourse.bass as bass
from concourse import mybir

F32 = mybir.dt.float32
F32R = mybir.dt.float32r
I32 = mybir.dt.int32
ALU = mybir.AluOpType
ACT = mybir.ActivationFunctionType
AX_X = mybir.AxisListType.X

P = 128
BATCHES, QUERIES, KEYS, D = 4, 1024, 64, 256
HEADS = 16
DK = D // HEADS
CHUNK = 512
TILES = CHUNK // P
PER_BATCH = QUERIES // CHUNK
CHUNKS = BATCHES * PER_BATCH
PAIRS = HEADS // 2
PC = D // P
QB = 8
QN = CHUNK // QB
SCALE = float(DK) ** -0.5
BIG = 2.0 ** 100
EPS = 1e-5
NQ = 3
NP_ = 3

MAX_SLOTS = {0: (0, 2), 2: (0, 3), 5: (1, 0), 7: (1, 1)}
FIRST_MAX_SLOTS = {0: (0, 0), 1: (0, 1), 2: (0, 2), 3: (0, 3), 5: (1, 0), 7: (1, 1)}
Q_SLOTS = (0, 3)
FIRST_Q_SLOTS = (1, 3)

IDENT, ID64, HEAD, BLOCK, ONES = 0, P, P + KEYS, P + KEYS + 8, P + KEYS + 12
CONSTS = ONES + 2 * 32


def build(nc, xT, x, maskT, ctxT, wq, wk, wv, wo, bias_cols, bias_rows, consts, out):
    with ExitStack() as ctx:
        def sb(name, shape, dt=F32):
            return ctx.enter_context(nc.sbuf_tensor(name, shape, dt))

        def bank(name, n=1):
            return ctx.enter_context(nc.psum_tensor(name, [P, n, 512], F32))

        def sem(name):
            return ctx.enter_context(nc.semaphore(name))

        con = sb("con", [P, CONSTS])
        bcol = sb("bcol", [P, 4])
        brow = sb("brow", [P, 4, D])
        ctx_t = sb("ctx_t", [P, PC, BATCHES, 2, KEYS])
        wq_sb = sb("wq_sb", [P, PC, D])
        wk_sb = sb("wk_sb", [P, PC, D])
        wv_sb = sb("wv_sb", [P, PC, D])
        wo_sb = sb("wo_sb", [P, PC, D])
        wq_h = sb("wq_h", [P, PC, D], F32R)
        wq_l = sb("wq_l", [P, PC, D], F32R)
        kt = sb("kt", [P, 2, BATCHES, KEYS])
        k_h = sb("k_h", [P, 2, BATCHES, KEYS], F32R)
        k_l = sb("k_l", [P, 2, BATCHES, KEYS], F32R)
        keys_mask = sb("keys_mask", [P, 2, 2, 2, 256], F32R)
        keys_low = sb("keys_low", [P, 2, 2, 2, 256], F32R)
        keys_max = sb("keys_max", [P, 2, 2, 2, 256], F32R)
        v_bd = sb("v_bd", [P, BATCHES, PAIRS, 32])
        xt_sb = sb("xt_sb", [P, 2, PC, CHUNK])
        xt_h = sb("xt_h", [P, 2, PC, CHUNK], F32R)
        xt_l = sb("xt_l", [P, 2, PC, CHUNK], F32R)
        m_sb = sb("m_sb", [KEYS, 2, CHUNK], I32)
        q_high = sb("q_high", [P, NQ, 2, 2, CHUNK], F32R)
        q_low = sb("q_low", [P, NQ, 2, 2, CHUNK], F32R)
        nmax = sb("nmax", [P, 2, TILES, HEADS])
        probs = sb("probs", [P, NP_, CHUNK])
        cx = sb("cx", [P, 2, 2, CHUNK])
        den_sb = sb("den_sb", [P, 2, CHUNK])
        den_t = sb("den_t", [P, 2, QN])
        rec_t = sb("rec_t", [P, 2, QN])
        rec = sb("rec", [P, 2, 2, CHUNK])
        cn = sb("cn", [P, 2, 2, CHUNK])
        x_sb = sb("x_sb", [P, 3, TILES, D])
        xb = sb("xb", [P, 3, TILES, D])
        res = sb("res", [P, 2, TILES, D])
        stat = sb("stat", [P, 2, TILES, 6])
        mv = sb("mv", [P, 2, TILES, 2])
        veps = sb("veps", [P, 2, TILES])
        rstd = sb("rstd", [P, 2, TILES])
        nmean = sb("nmean", [P, 2, TILES])
        shift = sb("shift", [P, 2, TILES])
        half_neg = sb("half_neg", [P, TILES])
        y = sb("y", [P, 2, TILES, D])

        rec_dram = nc.dram_tensor("rec_dram", (2, P, QN), F32, kind="Internal").ap()

        ps_max = bank("ps_max", 2)
        ps_s = bank("ps_s", 2)
        ps_c = bank("ps_c")
        ps_d = bank("ps_d")
        ps_q = bank("ps_q")
        ps_o = bank("ps_o")

        in_con, in_ctx, in_wk, in_wq, in_wv, in_wo, in_rows = (sem(n) for n in (
            "in_con", "in_ctx", "in_wk", "in_wq", "in_wv", "in_wo", "in_rows"))
        in_xt = [sem(f"in_xt{i}") for i in range(2)]
        in_mask = [sem(f"in_mask{i}") for i in range(2)]
        in_x = [sem(f"in_x{i}") for i in range(3)]
        k_done, v_done = sem("k_done"), sem("v_done")
        q_done, max_done, turn_done = sem("q_done"), sem("max_done"), sem("turn_done")
        s_done, pv_done, o_done = sem("s_done"), sem("pv_done"), sem("o_done")
        wqh_done, kh_done, kfix_done, kmax_done = sem("wqh_done"), sem("kh_done"), sem("kfix_done"), sem("kmax_done")
        xh_done, h_done, e_done, neg_done = sem("xh_done"), sem("h_done"), sem("e_done"), sem("neg_done")
        cx_done, den_done, y_done = sem("cx_done"), sem("den_done"), sem("y_done")
        wql_done, kt_done, kblk_done, vbd_done = (sem(n) for n in (
            "wql_done", "kt_done", "kblk_done", "vbd_done"))
        xl_done, mask_done, l_done, nm_done = sem("xl_done"), sem("mask_done"), sem("l_done"), sem("nm_done")
        rec_done, cn_done, res_done, bn_done, mv_done = (sem(n) for n in (
            "rec_done", "cn_done", "res_done", "bn_done", "mv_done"))
        fill_done, kl_done, klow_done, xb_done, ln_done, gam_done, bet_done = (sem(n) for n in (
            "fill_done", "kl_done", "klow_done", "xb_done", "ln_done", "gam_done", "bet_done"))
        den_in = [sem(f"den_in{i}") for i in range(2)]
        rec_out = [sem(f"rec_out{i}") for i in range(2)]
        rec_in = [sem(f"rec_in{i}") for i in range(2)]
        stored = [sem(f"stored{i}") for i in range(2)]

        def region(p):
            return p // 4, (p // 2) % 2, p % 2

        def rows(half):
            return slice(64 * half, 64 * half + 64)

        def query_bank(n):
            return {1: ps_d, 3: ps_c}.get(n, ps_q)

        def max_bank(c, t):
            return ps_s if c == 0 and t % 2 else ps_max

        def next_batch(step):
            b = step // PER_BATCH + 1
            return b if step % PER_BATCH == PER_BATCH - 1 and b < BATCHES else None

        def max_tiles(step, slot):
            ahead = (FIRST_MAX_SLOTS if step == 1 else MAX_SLOTS).get(slot)
            return (step + ahead[0], ahead[1]) if ahead and step + ahead[0] < CHUNKS else None

        REC_DMAS, DEN_DMAS = 2, 4

        block = ctx.enter_context(nc.Block())

        @block.sync
        def _(sp):
            def load_xt(c):
                if c >= 2:
                    sp.wait_ge(xl_done, c - 1)
                    sp.wait_ge(xh_done, c - 1)
                sp.dma_start(xt_sb[:, c % 2], xT[c]).then_inc(in_xt[c % 2], 16)

            def load_mask(c):
                if c >= 2:
                    sp.wait_ge(mask_done, 2 * (c - 1))
                sp.dma_start(m_sb[:, c % 2], maskT[c]).then_inc(in_mask[c % 2], 16)

            def load_x(c):
                if c >= 3:
                    sp.wait_ge(xb_done, c - 2)
                sp.dma_start(x_sb[:, c % 3], x[c]).then_inc(in_x[c % 3], 16)

            def spread_denominators(c):
                sp.wait_ge(den_done, c + 1)
                if c >= 2:
                    sp.wait_ge(rec_done, c - 1)
                for quad in range(4):
                    sp.dma_start(den_t[32 * quad:32 * quad + 32, c % 2],
                                 den_sb[32 * quad:32 * quad + 4, c % 2].rearrange("r (b n) -> r b n", b=QB)
                                 ).then_inc(den_in[c % 2], 16)

            def broadcast_reciprocals(c):
                sp.wait_ge(rec_done, c + 1)
                if c >= 2:
                    sp.wait_ge(cn_done, 2 * (c - 1))
                sp.dma_start(rec_dram[c % 2], rec_t[:, c % 2]).then_inc(rec_out[c % 2], 16)
                sp.wait_ge(rec_out[c % 2], 16 * (c // 2 + 1))
                for j in range(2):
                    sp.dma_start(rec[:, c % 2, j],
                                 rec_dram[c % 2].rearrange("(g j b) n -> g j (b n)", j=2, b=QB)[:, j]
                                 .unsqueeze(1).to_broadcast([8, DK, CHUNK])).then_inc(rec_in[c % 2], 16)

            def store(c):
                sp.wait_ge(bet_done, c + 1)
                sp.dma_start(out[c], y[:, c % 2]).then_inc(stored[c % 2], 16)

            sp.dma_start(wq_sb[:], wq).then_inc(in_wq, 16)
            load_xt(0)
            sp.dma_start(ctx_t[:], ctxT).then_inc(in_ctx, 16)
            sp.dma_start(wk_sb[:], wk).then_inc(in_wk, 16)
            sp.dma_start(con[:], consts).then_inc(in_con, 16)
            sp.dma_start(bcol[:], bias_cols).then_inc(in_con, 16)
            load_mask(0)
            load_xt(1)
            sp.dma_start(wv_sb[:], wv).then_inc(in_wv, 16)
            sp.dma_start(brow[:], bias_rows.to_broadcast([P, 4, D])).then_inc(in_rows, 16)
            load_mask(1)
            load_xt(2)
            load_mask(2)
            load_x(0)
            sp.dma_start(wo_sb[:], wo).then_inc(in_wo, 16)
            load_x(1)
            for step in range(1, CHUNKS + 3):
                if step + 2 < CHUNKS:
                    load_xt(step + 2)
                    load_mask(step + 2)
                if step + 1 < CHUNKS:
                    load_x(step + 1)
                if 0 <= step - 2 < CHUNKS:
                    spread_denominators(step - 2)
                if 0 <= step - 2 < CHUNKS:
                    broadcast_reciprocals(step - 2)
                if 0 <= step - 4 < CHUNKS:
                    store(step - 4)
            store(CHUNKS - 1)
            for c in (CHUNKS - 2, CHUNKS - 1):
                sp.wait_ge(stored[c % 2], 16 * (c // 2 + 1))

        @block.tensor
        def _(pe):
            def project_keys():
                pe.wait_ge(in_ctx, 16)
                pe.wait_ge(in_wk, 16)
                for j in range(2):
                    for d in range(PC):
                        mm = pe.matmul(ps_max[:, j, 0:256], wk_sb[:, d, j * P:(j + 1) * P],
                                       ctx_t[:, d, :, 0, :], start=d == 0, stop=d == PC - 1)
                mm.then_inc(k_done, 1)

            def project_values():
                pe.wait_ge(in_wv, 16)
                for b in range(BATCHES):
                    for d in range(PC):
                        mm = pe.matmul(ps_max[:, b // 2, (b % 2) * 256:(b % 2) * 256 + 256],
                                       ctx_t[:, d, b], wv_sb[:, d], start=d == 0, stop=d == PC - 1)
                mm.then_inc(v_done, 1)

            def project_queries(c, j):
                pe.wait_ge(xh_done, c + 1)
                n = 2 * c + j
                if n == 0:
                    pe.wait_ge(wqh_done, 1)
                elif n not in (1, 3):
                    pe.wait_ge(l_done, {2: 2, 4: 6}.get(n, 2 * n))
                for w, a in ((wq_h, xt_h), (wq_l, xt_h), (wq_h, xt_l)):
                    if w is wq_l and n == 0:
                        pe.wait_ge(wql_done, 1)
                    if a is xt_l:
                        pe.wait_ge(xl_done, c + 1)
                    for d in range(PC):
                        mm = pe.matmul(query_bank(n)[:, 0], w[:, d, j * P:(j + 1) * P], a[:, c % 2, d],
                                       start=d == 0 and w is wq_h and a is xt_h,
                                       stop=d == PC - 1 and a is xt_l)
                mm.then_inc(q_done, 1)

            def max_scores(c, t):
                n = TILES * c + t
                b = c // PER_BATCH
                s = b % 2
                if t == 0:
                    pe.wait_ge(h_done, 4 * (c + 1))
                    pe.wait_ge(mask_done, 2 * (c + 1))
                    pe.wait_ge(kblk_done, 2 * (b + 1))
                    pe.wait_ge(kfix_done, 2 if b == 0 else 8)
                    if c == 0:
                        pe.wait_ge(kt_done, 2)
                    if c == 1:
                        pe.wait_ge(vbd_done, 2 * BATCHES)
                if c:
                    pe.wait_ge(nm_done, n)
                elif t >= 2:
                    pe.wait_ge(nm_done, n - 1)
                for half in range(2):
                    for j in range(2):
                        g = 2 * half + j
                        mm = pe.matmul(max_bank(c, t)[:, g // 2, (g % 2) * 256:(g % 2) * 256 + 256],
                                       q_high[:, c % NQ, half, j, t * P:(t + 1) * P],
                                       keys_mask[:, s, half, j], start=True, stop=True)
                mm.then_inc(max_done, 1)

            def turn_max(c):
                pe.wait_ge(nm_done, TILES * (c + 1))
                if c >= 3:
                    pe.wait_ge(res_done, 2 * (c - 2))
                if c == 0:
                    pe.wait_ge(in_con, 32)
                for t in range(TILES):
                    mm = pe.transpose(ps_o[0:HEADS, 0, t * P:(t + 1) * P], nmax[:, c % 2, t],
                                      con[:, IDENT:IDENT + P])
                mm.then_inc(turn_done, 1)

            def scores(c, p):
                k = PAIRS * c + p
                j, half, pp = region(p)
                s = (c // PER_BATCH) % 2
                if k >= 2:
                    pe.wait_ge(e_done, k - 1)
                if p == 0:
                    pe.wait_ge(kmax_done, 2 * (c // PER_BATCH + 1))
                    pe.wait_ge(klow_done, 2 * (c // PER_BATCH + 1))
                    if c == 0:
                        pe.wait_ge(kfix_done, 4)
                    pe.wait_ge(l_done, 4 * (c + 1))
                lo, hi = pp * P, pp * P + P
                pe.matmul(ps_s[:, k % 2], keys_mask[:, s, half, j, lo:hi], q_high[:, c % NQ, half, j],
                          start=True, stop=False)
                pe.matmul(ps_s[:, k % 2], keys_low[:, s, half, j, lo:hi], q_high[:, c % NQ, half, j],
                          start=False, stop=False)
                if p == 0:
                    pe.wait_ge(neg_done, 2 * (c + 1))
                pe.matmul(ps_s[:, k % 2], keys_max[:, s, half, j, lo:hi], q_low[:, c % NQ, half, j],
                          start=False, stop=True).then_inc(s_done, 1)

            def values(k):
                c, p = divmod(k, PAIRS)
                b = c // PER_BATCH
                j, quad = p // 4, p % 4
                pe.wait_ge(e_done, k + 1)
                if k == 0:
                    pe.wait_ge(vbd_done, 2 * BATCHES)
                    pe.wait_ge(l_done, 8)
                if quad == 0 and 2 * c + j >= 1:
                    pe.wait_ge(cx_done, 2 * c + j)
                pe.matmul(ps_c[32 * quad:32 * quad + 32, 0], v_bd[:, b, p], probs[:, k % NP_],
                          start=True, stop=True)
                if p == 0 and c >= 1:
                    pe.wait_ge(den_done, c)
                pe.matmul(ps_d[32 * quad:32 * quad + 32, 0], con[:, ONES + 32 * j:ONES + 32 * j + 32],
                          probs[:, k % NP_], start=j == 0, stop=j == 1,
                          skip_group_check=True).then_inc(pv_done, 1)

            def output(c, i):
                if c == 0 and i == 0:
                    pe.wait_ge(in_wo, 16)
                pe.wait_ge(cn_done, 2 * (c + 1))
                if i == 0:
                    pe.wait_ge(res_done, 2 * c) if c else None
                    pe.wait_ge(neg_done, 2 * min(c + 3, CHUNKS))
                else:
                    pe.wait_ge(res_done, 2 * c + 1)
                for t in range(2):
                    for j in range(PC):
                        mm = pe.matmul(ps_o[:, 0, t * 256:t * 256 + 256],
                                       cn[:, c % 2, j, (2 * i + t) * P:(2 * i + t + 1) * P], wo_sb[:, j],
                                       start=j == 0, stop=j == PC - 1)
                mm.then_inc(o_done, 1)

            project_queries(0, 0)
            project_keys()
            project_queries(0, 1)
            max_scores(0, 0)
            max_scores(0, 1)
            project_queries(1, 0)
            max_scores(0, 2)
            max_scores(0, 3)
            project_queries(1, 1)
            turn_max(0)
            project_values()
            for step in range(1, CHUNKS + 3):
                front, back, last = step, step - 1, step - 2
                q_slots = FIRST_Q_SLOTS if step == 1 else Q_SLOTS
                for slot in range(PAIRS):
                    k = PAIRS * back + slot
                    if 0 <= back < CHUNKS:
                        scores(back, slot)
                    if 0 <= k - 1 < PAIRS * CHUNKS:
                        values(k - 1)
                    if slot in q_slots and front + 1 < CHUNKS:
                        project_queries(front + 1, q_slots.index(slot))
                    if max_tiles(step, slot):
                        max_scores(*max_tiles(step, slot))
                    if slot == 4 and front < CHUNKS:
                        turn_max(front)
                    if slot == 7 and 0 <= last < CHUNKS:
                        output(last, 0)
                    if slot == 1 and 0 <= step - 3 < CHUNKS:
                        output(step - 3, 1)

        @block.scalar
        def _(act):
            def high_x(c):
                act.wait_ge(in_xt[c % 2], 16 * (c // 2 + 1))
                if c >= 2:
                    act.wait_ge(q_done, 2 * (c - 1))
                act.activation(xt_h[:, c % 2], xt_sb[:, c % 2], ACT.Copy).then_inc(xh_done, 1)

            def high_queries(c, j):
                act.wait_ge(q_done, 2 * c + j + 1)
                if c >= NQ:
                    act.wait_ge(s_done, PAIRS * (c - NQ + 1))
                for half in range(2):
                    act.activation(q_high[rows(half), c % NQ, half, j], query_bank(2 * c + j)[rows(half), 0], ACT.Identity,
                                   bias=bcol[rows(half), j:j + 1]).then_inc(h_done, 1)

            def fixed_mask_rows(s):
                act.wait_ge(in_con, 32)
                for half in range(2):
                    other = rows(1 - half)
                    act.activation(keys_mask[other, s, half].rearrange("p j (h k) -> p (j h) k", k=KEYS),
                                   con[other, ID64:ID64 + KEYS].unsqueeze(1).to_broadcast([64, 8, KEYS]),
                                   ACT.Copy).then_inc(kfix_done, 1)

            def fixed_max_rows(s):
                for half in range(2):
                    other = rows(1 - half)
                    act.activation(keys_max[other, s, half].rearrange("p j (h k) -> p (j h) k", k=KEYS),
                                   con[other, ID64 + 8 * half:ID64 + 8 * half + 8].unsqueeze(2).to_broadcast([64, 8, KEYS]),
                                   ACT.Copy).then_inc(kfix_done, 1)

            def max_block(b, half):
                act.wait_ge(kblk_done, 2 * b + half + 1)
                if b >= 2:
                    act.wait_ge(s_done, PAIRS * PER_BATCH * (b - 1))
                act.activation(keys_max[rows(half), b % 2, half], keys_mask[rows(half), b % 2, half].bitcast(F32),
                               ACT.Copy).then_inc(kmax_done, 1)

            def exponentials(k):
                act.wait_ge(s_done, k + 1)
                if k >= NP_:
                    act.wait_ge(pv_done, k - NP_ + 1)
                act.activation(probs[:, k % NP_], ps_s[:, k % 2], ACT.Exp).then_inc(e_done, 1)

            def negative_max(c):
                act.wait_ge(turn_done, c + 1)
                if c in (0, 2):
                    act.wait_ge(fill_done, 2 if c == 0 else 4)
                if c >= NQ:
                    act.wait_ge(s_done, PAIRS * (c - NQ + 1))
                for half in range(2):
                    o = 64 * (1 - half)
                    act.activation(q_low[o:o + HEADS, c % NQ, half],
                                   ps_o[0:HEADS, 0].unsqueeze(1).to_broadcast([HEADS, 2, CHUNK]),
                                   ACT.Copy).then_inc(neg_done, 1)

            def context_out(c, j):
                act.wait_ge(pv_done, PAIRS * c + 4 * j + 4)
                if c >= 2:
                    act.wait_ge(cn_done, 2 * (c - 1))
                act.activation(cx[:, c % 2, j], ps_c[:, 0], ACT.Copy).then_inc(cx_done, 1)

            def denominators_out(c):
                act.wait_ge(pv_done, PAIRS * (c + 1))
                if c >= 2:
                    act.wait_ge(den_in[c % 2], 16 * DEN_DMAS * (c // 2))
                act.activation(den_sb[:, c % 2], ps_d[:, 0], ACT.Copy).then_inc(den_done, 1)

            def normalised(c, t):
                act.wait_ge(ln_done, 4 * (c + 1))
                if c >= 2:
                    act.wait_ge(stored[c % 2], 16 * (c // 2))
                act.activation(y[:, c % 2, t], res[:, c % 2, t], ACT.Identity, bias=shift[:, c % 2, t:t + 1],
                               scale=rstd[:, c % 2, t:t + 1]).then_inc(y_done, 1)

            act.wait_ge(in_wq, 16)
            act.activation(wq_h[:], wq_sb[:], ACT.Copy).then_inc(wqh_done, 1)
            high_x(0)
            high_x(1)
            high_queries(0, 0)
            act.wait_ge(kt_done, 2)
            act.activation(k_h[:], kt[:], ACT.Copy).then_inc(kh_done, 1)
            fixed_mask_rows(0)
            fixed_max_rows(0)
            high_queries(0, 1)
            max_block(0, 0)
            max_block(0, 1)
            high_queries(1, 0)
            high_queries(1, 1)
            negative_max(0)
            high_x(2)
            for step in range(1, CHUNKS + 3):
                front, back, last, norm = step, step - 1, step - 2, step - 3
                q_slots = FIRST_Q_SLOTS if step == 1 else Q_SLOTS
                for slot in range(PAIRS):
                    if 0 <= back < CHUNKS:
                        exponentials(PAIRS * back + slot)
                    if slot == 0 and 0 <= last < CHUNKS:
                        context_out(last, 1)
                        denominators_out(last)
                    if slot == 4 and 0 <= back < CHUNKS:
                        context_out(back, 0)
                    if step == 1 and slot == 0:
                        fixed_mask_rows(1)
                        fixed_max_rows(1)
                    if slot - 1 in q_slots and front + 1 < CHUNKS:
                        high_queries(front + 1, q_slots.index(slot - 1))
                    if slot == 2 and front + 2 < CHUNKS:
                        high_x(front + 2)
                    if slot in (3, 6) and next_batch(step):
                        max_block(next_batch(step), slot // 6)
                    if slot == 5 and front < CHUNKS:
                        negative_max(front)
                    if slot >= 4 and 0 <= norm < CHUNKS:
                        normalised(norm, slot - 4)

        @block.vector
        def _(dve):
            def low_x(c):
                dve.wait_ge(xh_done, c + 1)
                if c >= 2:
                    dve.wait_ge(q_done, 2 * (c - 1))
                dve.tensor_tensor(xt_l[:, c % 2], xt_sb[:, c % 2], xt_h[:, c % 2].bitcast(F32),
                                  ALU.subtract).then_inc(xl_done, 1)

            def mask_rows(c):
                dve.wait_ge(in_mask[c % 2], 16 * (c // 2 + 1))
                if c >= NQ:
                    dve.wait_ge(s_done, PAIRS * (c - NQ + 1))
                for half in range(2):
                    dve.tensor_scalar(q_high[rows(1 - half), c % NQ, half],
                                      m_sb[:, c % 2].unsqueeze(1).to_broadcast([KEYS, 2, CHUNK]),
                                      0.0, -BIG, ALU.is_equal, ALU.mult).then_inc(mask_done, 1)

            def low_queries(c, j):
                if c >= NQ:
                    dve.wait_ge(s_done, PAIRS * (c - NQ + 1))
                for half in range(2):
                    dve.wait_ge(h_done, 4 * c + 2 * j + half + 1)
                    dve.scalar_tensor_tensor(q_low[rows(half), c % NQ, half, j], query_bank(2 * c + j)[rows(half), 0],
                                             bcol[rows(half), j:j + 1],
                                             q_high[rows(half), c % NQ, half, j].bitcast(F32),
                                             ALU.add, ALU.subtract).then_inc(l_done, 1)

            def maxima(c, t):
                dve.wait_ge(max_done, TILES * c + t + 1)
                if c >= 2:
                    dve.wait_ge(turn_done, c - 1)
                dve.tensor_reduce(nmax[:, c % 2, t], max_bank(c, t)[:].rearrange("p a (h k) -> p (a h) k", k=KEYS),
                                  AX_X, ALU.max, negate=True).then_inc(nm_done, 1)

            def high_blocks(b, half):
                if b >= 2:
                    dve.wait_ge(s_done, PAIRS * PER_BATCH * (b - 1))
                r = rows(half)
                for j in range(2):
                    blk = dve.tensor_tensor(keys_mask[r, b % 2, half, j].rearrange("p (h k) -> p h k", k=KEYS),
                                            k_h[r, j, b].bitcast(F32).unsqueeze(1).to_broadcast([64, 4, KEYS]),
                                            con[r, BLOCK:BLOCK + 4].unsqueeze(2).to_broadcast([64, 4, KEYS]),
                                            ALU.mult)
                blk.then_inc(kblk_done, 1)

            def reciprocals(c):
                dve.wait_ge(den_in[c % 2], 16 * DEN_DMAS * (c // 2 + 1))
                if c >= 2:
                    dve.wait_ge(rec_in[c % 2], 16 * REC_DMAS * (c // 2))
                dve.reciprocal(rec_t[:, c % 2], den_t[:, c % 2]).then_inc(rec_done, 1)

            def divide(c):
                dve.wait_ge(rec_in[c % 2], 16 * REC_DMAS * (c // 2 + 1))
                dve.wait_ge(cx_done, 2 * (c + 1))
                if c >= 2:
                    dve.wait_ge(o_done, 2 * (c - 1))
                for j in range(2):
                    dve.tensor_tensor(cn[:, c % 2, j], cx[:, c % 2, j], rec[:, c % 2, j],
                                      ALU.mult).then_inc(cn_done, 1)

            def residual(c, i):
                dve.wait_ge(o_done, 2 * c + i + 1)
                dve.wait_ge(xb_done, c + 1)
                if c >= 2:
                    dve.wait_ge(y_done, TILES * (c - 1))
                two = slice(2 * i, 2 * i + 2)
                dve.tensor_tensor(res[:, c % 2, two], ps_o[:, 0].rearrange("p (t d) -> p t d", t=2),
                                  xb[:, c % 3, two], ALU.add).then_inc(res_done, 1)

            def moments(c, i):
                n = 2 * c + i + 1
                dve.wait_ge(res_done, n)
                if c >= 2:
                    dve.wait_ge(ln_done, 4 * (c - 1))
                for t in (2 * i, 2 * i + 1):
                    dve.bn_stats(stat[:, c % 2, t], res[:, c % 2, t]).then_inc(bn_done, 1)
                dve.wait_ge(bn_done, 2 * n)
                for t in (2 * i, 2 * i + 1):
                    dve.bn_aggr(mv[:, c % 2, t], stat[:, c % 2, t]).then_inc(mv_done, 1)

            dve.wait_ge(wqh_done, 1)
            dve.tensor_tensor(wq_l[:], wq_sb[:], wq_h[:].bitcast(F32), ALU.subtract).then_inc(wql_done, 1)
            low_x(0)
            low_x(1)
            dve.wait_ge(in_con, 32)
            dve.wait_ge(k_done, 1)
            for j in range(2):
                dve.tensor_scalar(kt[:, j], ps_max[:, j, 0:256].rearrange("p (b k) -> p b k", k=KEYS),
                                  bcol[:, 2 + j:3 + j], SCALE, ALU.add, ALU.mult).then_inc(kt_done, 1)
            mask_rows(0)
            dve.wait_ge(fill_done, 2)
            low_queries(0, 0)
            dve.wait_ge(kh_done, 1)
            high_blocks(0, 0)
            high_blocks(0, 1)
            low_queries(0, 1)
            for t in range(TILES):
                maxima(0, t)
            low_queries(1, 0)
            low_queries(1, 1)
            dve.wait_ge(v_done, 1)
            dve.wait_ge(fill_done, 3)
            dve.wait_ge(in_rows, 16)
            for b in range(BATCHES):
                for h in range(2):
                    r = rows(h)
                    dve.tensor_tensor(
                        v_bd[r, b, :, 16 * h:16 * h + 16],
                        ps_max[r, b // 2, (b % 2) * 256:(b % 2) * 256 + 256].rearrange(
                            "k (p e) -> k p e", e=32)[:, :, 16 * h:16 * h + 16],
                        brow[r, 0].rearrange("k (p e) -> k p e", e=32)[:, :, 16 * h:16 * h + 16],
                        ALU.add).then_inc(vbd_done, 1)
            mask_rows(1)
            low_x(2)
            dve.wait_ge(fill_done, 4)
            for step in range(1, CHUNKS + 3):
                front, last, norm = step, step - 2, step - 3
                q_slots = FIRST_Q_SLOTS if step == 1 else Q_SLOTS
                for slot in range(PAIRS):
                    if slot == 0 and 0 <= norm < CHUNKS:
                        residual(norm, 0)
                        moments(norm, 0)
                    if slot == 2 and 0 <= norm < CHUNKS:
                        residual(norm, 1)
                        moments(norm, 1)
                    if slot - 1 == q_slots[0] and front + 1 < CHUNKS:
                        low_queries(front + 1, 0)
                    if slot < 5 and max_tiles(step, slot):
                        maxima(*max_tiles(step, slot))
                    if slot in (2, 3) and next_batch(step):
                        high_blocks(next_batch(step), slot - 2)
                    if slot == 3 and front + 1 < CHUNKS:
                        mask_rows(front + 1)
                    if slot == 3 and 0 <= last < CHUNKS:
                        reciprocals(last)
                    if slot == 4 and front + 1 < CHUNKS:
                        low_queries(front + 1, 1)
                    if slot == 5 and front + 2 < CHUNKS:
                        low_x(front + 2)
                    if slot == 5 and max_tiles(step, slot):
                        maxima(*max_tiles(step, slot))
                    if slot == 6 and 0 <= last < CHUNKS:
                        divide(last)
                    if slot == 7 and max_tiles(step, slot):
                        maxima(*max_tiles(step, slot))

        @block.gpsimd
        def _(pool):
            def with_bias(c):
                pool.wait_ge(in_x[c % 3], 16 * (c // 3 + 1))
                if c >= 3:
                    pool.wait_ge(res_done, 2 * (c - 2))
                pool.tensor_tensor(xb[:, c % 3], x_sb[:, c % 3],
                                   brow[:, 1].unsqueeze(1).to_broadcast([P, TILES, D]), ALU.add).then_inc(xb_done, 1)

            def low_blocks(b):
                if b >= 2:
                    pool.wait_ge(s_done, PAIRS * PER_BATCH * (b - 1))
                for j in range(2):
                    pool.tensor_tensor(
                        keys_low[:, b % 2, :, j].rearrange("p f (h k) -> p f h k", k=KEYS),
                        k_l[:, j, b].bitcast(F32).unsqueeze(1).unsqueeze(1).to_broadcast([P, 2, 4, KEYS]),
                        con[:, HEAD:HEAD + 8].rearrange("p (f h) -> p f h", f=2).unsqueeze(3)
                        .to_broadcast([P, 2, 4, KEYS]), ALU.mult).then_inc(klow_done, 1)

            def deviations(c):
                i = c % 2
                pool.wait_ge(mv_done, TILES * (c + 1))
                if c >= 2:
                    pool.wait_ge(y_done, TILES * (c - 1))
                pool.tensor_scalar(veps[:, i], mv[:, i, :, 1], EPS, 1.0, ALU.add, ALU.mult).then_inc(ln_done, 1)
                pool.tensor_scalar(nmean[:, i], mv[:, i, :, 0], -1.0, 0.0, ALU.mult, ALU.add).then_inc(ln_done, 1)
                pool.wait_ge(ln_done, 4 * c + 2)
                pool.tensor_tensor(rstd[:, i], veps[:, i], half_neg[:], ALU.pow).then_inc(ln_done, 1)
                pool.wait_ge(ln_done, 4 * c + 3)
                pool.tensor_tensor(shift[:, i], nmean[:, i], rstd[:, i], ALU.mult).then_inc(ln_done, 1)

            def affine(c):
                i = c % 2
                pool.wait_ge(y_done, TILES * (c + 1))
                pool.tensor_tensor(y[:, i], y[:, i], brow[:, 2].unsqueeze(1).to_broadcast([P, TILES, D]),
                                   ALU.mult).then_inc(gam_done, 1)
                pool.wait_ge(gam_done, c + 1)
                pool.tensor_tensor(y[:, i], y[:, i], brow[:, 3].unsqueeze(1).to_broadcast([P, TILES, D]),
                                   ALU.add).then_inc(bet_done, 1)

            pool.memset(half_neg[:], -0.5).then_inc(fill_done, 1)
            pool.memset(q_low[:, 0:2].bitcast(F32), 0.0).then_inc(fill_done, 1)
            pool.memset(v_bd[:], 0.0).then_inc(fill_done, 1)
            pool.memset(q_low[:, 2:NQ].bitcast(F32), 0.0).then_inc(fill_done, 1)
            pool.wait_ge(fill_done, 4)
            pool.wait_ge(kt_done, 2)
            pool.wait_ge(kh_done, 1)
            pool.tensor_tensor(k_l[:], kt[:], k_h[:].bitcast(F32), ALU.subtract).then_inc(kl_done, 1)
            pool.wait_ge(kl_done, 1)
            pool.wait_ge(in_con, 32)
            low_blocks(0)
            pool.wait_ge(in_rows, 16)
            for step in range(1, CHUNKS + 3):
                if 0 <= step - 1 < CHUNKS:
                    with_bias(step - 1)
                if 0 <= step - 3 < CHUNKS:
                    deviations(step - 3)
                if next_batch(step):
                    low_blocks(next_batch(step))
                if 0 <= step - 3 < CHUNKS:
                    affine(step - 3)


def kernel(x, ctx_1024, mask_BxSxS2_ik1, L0_xattn_w_q, L0_xattn_b_q, L0_xattn_w_k, L0_xattn_b_k, L0_xattn_w_v,
           L0_xattn_b_v, L0_xattn_w_o, L0_xattn_b_o, L0_xattn_ln_gamma, L0_xattn_ln_beta):
    import concourse.bacc as bacc
    from concourse.bass_utils import run_bass_kernel_spmd

    x, ctx, mask = (np.asarray(a) for a in (x, ctx_1024, mask_BxSxS2_ik1))

    def weight(w):
        return np.ascontiguousarray(np.asarray(w).T.reshape(PC, P, D).transpose(1, 0, 2))

    chunks = x.reshape(CHUNKS, CHUNK, D)
    consts = np.zeros((P, CONSTS), np.float32)
    row = np.arange(P)
    consts[row, IDENT + row] = 1
    consts[row, ID64 + row % 64] = 1
    consts[row, HEAD + row // DK] = 1
    consts[row, BLOCK + row % 64 // DK] = 1
    for j in range(2):
        consts[row, ONES + 32 * j + 2 * (row // 64) + j] = 1
    arrays = {
        "xT": np.ascontiguousarray(chunks.transpose(0, 2, 1).reshape(CHUNKS, PC, P, CHUNK).transpose(0, 2, 1, 3)),
        "x": np.ascontiguousarray(chunks.reshape(CHUNKS, TILES, P, D).transpose(0, 2, 1, 3)),
        "maskT": np.ascontiguousarray(mask.reshape(CHUNKS, CHUNK, KEYS).transpose(0, 2, 1)),
        "ctxT": np.ascontiguousarray(np.broadcast_to(
            ctx.transpose(2, 0, 1).reshape(PC, P, BATCHES, 1, KEYS), (PC, P, BATCHES, 2, KEYS)
        ).transpose(1, 0, 2, 3, 4)),
        "wq": weight(L0_xattn_w_q), "wk": weight(L0_xattn_w_k),
        "wv": weight(L0_xattn_w_v), "wo": weight(L0_xattn_w_o),
        "bias_cols": np.ascontiguousarray(np.concatenate(
            [np.asarray(b).reshape(PC, P).T for b in (L0_xattn_b_q, L0_xattn_b_k)], axis=1)),
        "bias_rows": np.stack([np.asarray(b) for b in (
            L0_xattn_b_v, L0_xattn_b_o, L0_xattn_ln_gamma, L0_xattn_ln_beta)])[None],
        "consts": consts,
    }
    nc = bacc.Bacc("TRN2", target_bir_lowering=False, num_devices=1)
    args = [nc.dram_tensor(n, a.shape, mybir.dt.from_np(a.dtype), kind="ExternalInput").ap()
            for n, a in arrays.items()]
    out = nc.dram_tensor("out", (CHUNKS, P, TILES, D), F32, kind="ExternalOutput").ap()
    build(nc, *args, out)
    r = run_bass_kernel_spmd(nc, [arrays], core_ids=[0])
    return r.results[0]["out"].transpose(0, 2, 1, 3).reshape(BATCHES, QUERIES, D)
```

```python
from contextlib import ExitStack

import numpy as np

import concourse.bass as bass
from concourse import mybir

F32 = mybir.dt.float32
F32R = mybir.dt.float32r
I32 = mybir.dt.int32
ALU = mybir.AluOpType
ACT = mybir.ActivationFunctionType
AX_X = mybir.AxisListType.X

P = 128
BATCHES, QUERIES, KEYS, D = 4, 1024, 64, 256
HEADS = 16
DK = D // HEADS
CHUNK = 512
TILES = CHUNK // P
PER_BATCH = QUERIES // CHUNK
CHUNKS = BATCHES * PER_BATCH
PAIRS = HEADS // 2
PC = D // P
QB = 8
QN = CHUNK // QB
SCALE = float(DK) ** -0.5
BIG = 2.0 ** 100
EPS = 1e-5
NQ = 3
NP_ = 3

MAX_SLOTS = {2: (0, 2), 4: (0, 3), 5: (1, 0), 7: (1, 1)}
FIRST_MAX_SLOTS = {1: (0, 0), 2: (0, 1), 3: (0, 2), 4: (0, 3), 5: (1, 0), 7: (1, 1)}
Q_SLOTS = (1, 3)
TURN_SLOT = 5
OUT_SLOTS = (0, 6)
LATE_VALUES_SLOT = 1
NORM_SLOTS = (4, 5, 5, 6)
MASK_SLOTS = (1, 2)
X_HIGH_SLOT = 2
X_LOW_SLOT = 4
RECIPROCAL_SLOT = 2
DIVIDE_SLOT = 6
KEY_SLOTS = (3, 4)
KEY_COPY_SLOTS = (4, 5)
LAST_OUT_SLOTS = (0, 3)
LAST_NORM_SLOTS = (1, 2, 3, 4)
LATE_NORM_SLOTS = (5, 6, 6, 7)

IDENT, ID64, HEAD, BLOCK, ONES = 0, P, P + KEYS, P + KEYS + 8, P + KEYS + 12
CONSTS = ONES + 2 * 32


def build(nc, xT, x, maskT, ctxT, wq, wk, wv, wo, bias_cols, bias_rows, consts, out):
    with ExitStack() as ctx:
        def sb(name, shape, dt=F32):
            return ctx.enter_context(nc.sbuf_tensor(name, shape, dt))

        def bank(name, n=1):
            return ctx.enter_context(nc.psum_tensor(name, [P, n, 512], F32))

        def sem(name):
            return ctx.enter_context(nc.semaphore(name))

        con = sb("con", [P, CONSTS])
        bcol = sb("bcol", [P, 4])
        brow = sb("brow", [P, 4, D])
        ctx_t = sb("ctx_t", [P, PC, BATCHES, 2, KEYS])
        wq_sb = sb("wq_sb", [P, PC, D])
        wk_sb = sb("wk_sb", [P, PC, D])
        wv_sb = sb("wv_sb", [P, PC, D])
        wo_sb = sb("wo_sb", [P, PC, D])
        wq_h = sb("wq_h", [P, PC, D], F32R)
        wq_l = sb("wq_l", [P, PC, D], F32R)
        kt = sb("kt", [P, 2, BATCHES, KEYS])
        k_h = sb("k_h", [P, 2, BATCHES, KEYS], F32R)
        k_l = sb("k_l", [P, 2, BATCHES, KEYS], F32R)
        keys_mask = sb("keys_mask", [P, 2, 2, 2, 256], F32R)
        keys_low = sb("keys_low", [P, 2, 2, 2, 256], F32R)
        keys_max = sb("keys_max", [P, 2, 2, 2, 256], F32R)
        v_bd = sb("v_bd", [P, BATCHES, PAIRS, 32])
        xt_sb = sb("xt_sb", [P, 2, PC, CHUNK])
        xt_h = sb("xt_h", [P, 2, PC, CHUNK], F32R)
        xt_l = sb("xt_l", [P, 2, PC, CHUNK], F32R)
        m_sb = sb("m_sb", [KEYS, 2, CHUNK], I32)
        q_high = sb("q_high", [P, NQ, 2, 2, CHUNK], F32R)
        q_low = sb("q_low", [P, NQ, 2, 2, CHUNK], F32R)
        nmax = sb("nmax", [P, 2, TILES, HEADS])
        probs = sb("probs", [P, NP_, CHUNK])
        cx = sb("cx", [P, 2, 2, CHUNK])
        den_sb = sb("den_sb", [P, 2, CHUNK])
        den_t = sb("den_t", [P, 2, QN])
        rec_t = sb("rec_t", [P, 2, QN])
        rec = sb("rec", [P, 2, 2, CHUNK])
        cn = sb("cn", [P, 2, 2, CHUNK])
        x_sb = sb("x_sb", [P, 3, TILES, D])
        xb = sb("xb", [P, 3, TILES, D])
        res = sb("res", [P, 2, TILES, D])
        stat = sb("stat", [P, 2, TILES, 6])
        mv = sb("mv", [P, 2, TILES, 2])
        veps = sb("veps", [P, 2, TILES])
        rstd = sb("rstd", [P, 2, TILES])
        nmean = sb("nmean", [P, 2, TILES])
        shift = sb("shift", [P, 2, TILES])
        half_neg = sb("half_neg", [P, TILES])
        y = sb("y", [P, 2, TILES, D])
        rec_q = sb("rec_q", [P, TILES, HEADS])

        rec_dram = nc.dram_tensor("rec_dram", (2, P, QN), F32, kind="Internal").ap()

        ps_max = bank("ps_max", 2)
        ps_s = bank("ps_s", 2)
        ps_c = bank("ps_c")
        ps_d = bank("ps_d")
        ps_q = bank("ps_q")
        ps_o = bank("ps_o")

        in_con, in_ctx, in_wk, in_wq, in_wv, in_wo, in_rows = (sem(n) for n in (
            "in_con", "in_ctx", "in_wk", "in_wq", "in_wv", "in_wo", "in_rows"))
        in_xt = [sem(f"in_xt{i}") for i in range(2)]
        in_mask = [sem(f"in_mask{i}") for i in range(2)]
        in_x = [sem(f"in_x{i}") for i in range(3)]
        k_done, v_done, dturn_done, spread_done = sem("k_done"), sem("v_done"), sem("dturn_done"), sem("spread_done")
        q_done, max_done, turn_done = sem("q_done"), sem("max_done"), sem("turn_done")
        s_done, pv_done, o_done = sem("s_done"), sem("pv_done"), sem("o_done")
        wqh_done, kh_done, kfix_done, kmax_done = sem("wqh_done"), sem("kh_done"), sem("kfix_done"), sem("kmax_done")
        xh_done, h_done, e_done, neg_done = sem("xh_done"), sem("h_done"), sem("e_done"), sem("neg_done")
        cx_done, den_done, y_done = sem("cx_done"), sem("den_done"), sem("y_done")
        wql_done, kt_done, kblk_done, vbd_done = (sem(n) for n in (
            "wql_done", "kt_done", "kblk_done", "vbd_done"))
        xl_done, mask_done, l_done, nm_done = sem("xl_done"), sem("mask_done"), sem("l_done"), sem("nm_done")
        rep_done = [sem(f"rep_done{j}") for j in range(2)]
        rq_done, last_gam_done, last_bet_done = sem("rq_done"), sem("last_gam_done"), sem("last_bet_done")
        rec_done, cn_done, res_done, bn_done, mv_done = (sem(n) for n in (
            "rec_done", "cn_done", "res_done", "bn_done", "mv_done"))
        fill_done, kl_done, klow_done, xb_done, ln_done, gam_done, bet_done = (sem(n) for n in (
            "fill_done", "kl_done", "klow_done", "xb_done", "ln_done", "gam_done", "bet_done"))
        den_in = [sem(f"den_in{i}") for i in range(2)]
        rec_out = [sem(f"rec_out{i}") for i in range(2)]
        rec_in = [sem(f"rec_in{i}") for i in range(2)]
        stored = [sem(f"stored{i}") for i in range(2)]

        def region(p):
            return p // 4, (p // 2) % 2, p % 2

        def rows(half):
            return slice(64 * half, 64 * half + 64)

        def query_bank(n):
            return {1: ps_d, 3: ps_c}.get(n, ps_q)

        def max_bank(c, t):
            return ps_s if c == 0 and t % 2 else ps_max

        def out_slots(step):
            return LAST_OUT_SLOTS if step == CHUNKS else OUT_SLOTS

        def y_of(c):
            return xt_sb[:, c % 2].rearrange("p a (t d) -> p (a t) d", d=D) if c == CHUNKS - 1 else y[:, c % 2]

        def value_bank(b):
            return (ps_c, ps_o)[b // 2]

        def out_tile(c, i):
            return ps_max[:, CHUNKS - 1 - c] if c >= CHUNKS - 2 and i == 1 else ps_o[:, 0]

        def turn_bank(c):
            return ps_o if c == 0 else ps_q

        def replicated(j):
            return (rec[:, (CHUNKS - 1) % 2, j].rearrange("p (t g d) -> p t g d", t=TILES, d=DK),
                    rec_q[:].rearrange("p t (g j) -> p t g j", j=2)[:, :, :, j].unsqueeze(3)
                    .to_broadcast([P, TILES, 8, DK]))

        def next_batch(step):
            b = step // PER_BATCH + 1
            return b if step % PER_BATCH == PER_BATCH - 1 and b < BATCHES else None

        def max_tiles(step, slot):
            ahead = (FIRST_MAX_SLOTS if step == 1 else MAX_SLOTS).get(slot)
            return (step + ahead[0], ahead[1]) if ahead and step + ahead[0] < CHUNKS else None

        REC_DMAS, DEN_DMAS = 2, 4

        block = ctx.enter_context(nc.Block())

        @block.sync
        def _(sp):
            def load_xt(c):
                if c >= 2:
                    sp.wait_ge(xl_done, c - 1)
                    sp.wait_ge(xh_done, c - 1)
                sp.dma_start(xt_sb[:, c % 2], xT[c]).then_inc(in_xt[c % 2], 16)

            def load_mask(c):
                if c >= 2:
                    sp.wait_ge(mask_done, 2 * (c - 1))
                sp.dma_start(m_sb[:, c % 2], maskT[c]).then_inc(in_mask[c % 2], 16)

            def load_x(c):
                if c >= 3:
                    sp.wait_ge(xb_done, c - 2)
                sp.dma_start(x_sb[:, c % 3], x[c]).then_inc(in_x[c % 3], 16)

            def spread_denominators(c):
                sp.wait_ge(den_done, c + 1)
                if c >= 2:
                    sp.wait_ge(rec_done, c - 1)
                for quad in range(4):
                    sp.dma_start(den_t[32 * quad:32 * quad + 32, c % 2],
                                 den_sb[32 * quad:32 * quad + 4, c % 2].rearrange("r (b n) -> r b n", b=QB)
                                 ).then_inc(den_in[c % 2], 16)

            def broadcast_reciprocals(c):
                sp.wait_ge(rec_done, c + 1)
                if c >= 2:
                    sp.wait_ge(cn_done, 2 * (c - 1))
                sp.dma_start(rec_dram[c % 2], rec_t[:, c % 2]).then_inc(rec_out[c % 2], 16)
                sp.wait_ge(rec_out[c % 2], 16 * (c // 2 + 1))
                for j in range(2):
                    sp.dma_start(rec[:, c % 2, j],
                                 rec_dram[c % 2].rearrange("(g j b) n -> g j (b n)", j=2, b=QB)[:, j]
                                 .unsqueeze(1).to_broadcast([8, DK, CHUNK])).then_inc(rec_in[c % 2], 16)

            def store(c):
                sp.wait_ge(bet_done, 2 * (c + 1))
                sp.dma_start(out[c], y_of(c)).then_inc(stored[c % 2], 16)

            def store_half(c, i):
                if (c, i) == (CHUNKS - 2, 0):
                    sp.wait_ge(bet_done, 2 * c + 1)
                else:
                    sp.wait_ge(last_bet_done, 2 * (c - CHUNKS + 2) + i)
                two = slice(2 * i, 2 * i + 2)
                sp.dma_start(out[c, :, two], y_of(c)[:, two]).then_inc(stored[c % 2], 16)

            sp.dma_start(wq_sb[:], wq).then_inc(in_wq, 16)
            load_xt(0)
            sp.dma_start(ctx_t[:], ctxT).then_inc(in_ctx, 16)
            sp.dma_start(wk_sb[:], wk).then_inc(in_wk, 16)
            sp.dma_start(con[:], consts).then_inc(in_con, 16)
            sp.dma_start(bcol[:], bias_cols).then_inc(in_con, 16)
            load_mask(0)
            load_xt(1)
            sp.dma_start(wv_sb[:], wv).then_inc(in_wv, 16)
            sp.dma_start(brow[:], bias_rows.to_broadcast([P, 4, D])).then_inc(in_rows, 16)
            load_mask(1)
            load_xt(2)
            load_mask(2)
            load_x(0)
            sp.dma_start(wo_sb[:], wo).then_inc(in_wo, 16)
            load_x(1)
            load_xt(3)
            for step in range(1, CHUNKS + 1):
                if step + 3 < CHUNKS:
                    load_xt(step + 3)
                if 3 <= step + 2 < CHUNKS:
                    load_mask(step + 2)
                if step + 1 < CHUNKS:
                    load_x(step + 1)
                if step >= 2:
                    spread_denominators(step - 2)
                    broadcast_reciprocals(step - 2)
                if step >= 4:
                    store(step - 4)
            store(CHUNKS - 3)
            for c, i in ((CHUNKS - 2, 1), (CHUNKS - 1, 0), (CHUNKS - 2, 0), (CHUNKS - 1, 1)):
                store_half(c, i)
            for c in (CHUNKS - 2, CHUNKS - 1):
                sp.wait_ge(stored[c % 2], 16 * (c // 2 + 2))

        @block.tensor
        def _(pe):
            def project_keys():
                pe.wait_ge(in_ctx, 16)
                pe.wait_ge(in_wk, 16)
                for j in range(2):
                    for d in range(PC):
                        mm = pe.matmul(ps_max[:, j, 0:256], wk_sb[:, d, j * P:(j + 1) * P],
                                       ctx_t[:, d, :, 0, :], start=d == 0, stop=d == PC - 1)
                mm.then_inc(k_done, 1)

            def project_values():
                pe.wait_ge(in_wv, 16)
                for b in range(BATCHES):
                    for d in range(PC):
                        mm = pe.matmul(value_bank(b)[:, 0, (b % 2) * 256:(b % 2) * 256 + 256],
                                       ctx_t[:, d, b], wv_sb[:, d], start=d == 0, stop=d == PC - 1)
                mm.then_inc(v_done, 1)

            def project_queries(c, j):
                pe.wait_ge(xh_done, c + 1)
                n = 2 * c + j
                if n == 0:
                    pe.wait_ge(wqh_done, 1)
                elif n == 3:
                    pe.wait_ge(vbd_done, 2)
                elif j == 0 and c >= 3:
                    pe.wait_ge(neg_done, 2 * (c - 1))
                elif n != 1:
                    pe.wait_ge(l_done, {2: 2, 4: 6}.get(n, 2 * n))
                for w, a in ((wq_h, xt_h), (wq_l, xt_h), (wq_h, xt_l)):
                    if w is wq_l and n == 0:
                        pe.wait_ge(wql_done, 1)
                    if a is xt_l:
                        pe.wait_ge(xl_done, c + 1)
                    for d in range(PC):
                        mm = pe.matmul(query_bank(n)[:, 0], w[:, d, j * P:(j + 1) * P], a[:, c % 2, d],
                                       start=d == 0 and w is wq_h and a is xt_h,
                                       stop=d == PC - 1 and a is xt_l)
                mm.then_inc(q_done, 1)

            def max_scores(c, t):
                n = TILES * c + t
                b = c // PER_BATCH
                s = b % 2
                if t == 0:
                    pe.wait_ge(h_done, 4 * (c + 1))
                    pe.wait_ge(mask_done, 2 * (c + 1))
                    pe.wait_ge(kblk_done, 2 * (b + 1))
                    pe.wait_ge(kfix_done, 2 if b == 0 else 6)
                    if c == 0:
                        pe.wait_ge(kt_done, 2)
                if c:
                    pe.wait_ge(nm_done, n)
                elif t >= 2:
                    pe.wait_ge(nm_done, n - 1)
                for half in range(2):
                    for j in range(2):
                        g = 2 * half + j
                        mm = pe.matmul(max_bank(c, t)[:, g // 2, (g % 2) * 256:(g % 2) * 256 + 256],
                                       q_high[:, c % NQ, half, j, t * P:(t + 1) * P],
                                       keys_mask[:, s, half, j], start=True, stop=True)
                mm.then_inc(max_done, 1)

            def turn_max(c):
                pe.wait_ge(nm_done, TILES * (c + 1))
                if c == 0:
                    pe.wait_ge(in_con, 32)
                    pe.wait_ge(vbd_done, 4)
                elif c + 1 < CHUNKS:
                    pe.wait_ge(l_done, 4 * (c + 2))
                else:
                    pe.wait_ge(neg_done, 2 * c)
                for t in range(TILES):
                    mm = pe.transpose(turn_bank(c)[0:HEADS, 0, t * P:(t + 1) * P], nmax[:, c % 2, t],
                                      con[:, IDENT:IDENT + P])
                mm.then_inc(turn_done, 1)

            def scores(c, p):
                k = PAIRS * c + p
                j, half, pp = region(p)
                s = (c // PER_BATCH) % 2
                if k >= 2:
                    pe.wait_ge(e_done, k - 1)
                if p == 0:
                    pe.wait_ge(kmax_done, 2 * (c // PER_BATCH + 1))
                    pe.wait_ge(klow_done, 2 * (c // PER_BATCH + 1))
                    pe.wait_ge(kfix_done, 4 if c < PER_BATCH else 8)
                    pe.wait_ge(l_done, 4 * (c + 1))
                lo, hi = pp * P, pp * P + P
                pe.matmul(ps_s[:, k % 2], keys_mask[:, s, half, j, lo:hi], q_high[:, c % NQ, half, j],
                          start=True, stop=False)
                pe.matmul(ps_s[:, k % 2], keys_low[:, s, half, j, lo:hi], q_high[:, c % NQ, half, j],
                          start=False, stop=False)
                if p in (0, 2):
                    pe.wait_ge(neg_done, 2 * c + half + 1)
                pe.matmul(ps_s[:, k % 2], keys_max[:, s, half, j, lo:hi], q_low[:, c % NQ, half, j],
                          start=False, stop=True).then_inc(s_done, 1)

            def values(k):
                c, p = divmod(k, PAIRS)
                b = c // PER_BATCH
                j, quad = p // 4, p % 4
                pe.wait_ge(e_done, k + 1)
                if k == 0:
                    pe.wait_ge(vbd_done, 4)
                    pe.wait_ge(l_done, 8)
                if quad == 0 and 2 * c + j >= 1:
                    pe.wait_ge(cx_done, 2 * c + j)
                pe.matmul(ps_c[32 * quad:32 * quad + 32, 0], v_bd[:, b, p], probs[:, k % NP_],
                          start=True, stop=True)
                if p == 0 and c >= 1:
                    pe.wait_ge(den_done, c)
                pe.matmul(ps_d[32 * quad:32 * quad + 32, 0], con[:, ONES + 32 * j:ONES + 32 * j + 32],
                          probs[:, k % NP_], start=j == 0, stop=j == 1,
                          skip_group_check=True).then_inc(pv_done, 1)

            def output(c, i):
                if c == 0 and i == 0:
                    pe.wait_ge(in_wo, 16)
                pe.wait_ge(cn_done, 2 * (c + 1))
                if c == 0 and i == 0:
                    pe.wait_ge(neg_done, 2)
                elif c == CHUNKS - 2 and i == 1:
                    pe.wait_ge(nm_done, TILES * CHUNKS)
                elif c == CHUNKS - 1 and i == 1:
                    pe.wait_ge(rq_done, 1)
                elif c == CHUNKS - 1:
                    pe.wait_ge(res_done, 2 * c - 1)
                else:
                    pe.wait_ge(res_done, 2 * c + i)
                for t in range(2):
                    for j in range(PC):
                        mm = pe.matmul(out_tile(c, i)[:, t * 256:t * 256 + 256],
                                       cn[:, c % 2, j, (2 * i + t) * P:(2 * i + t + 1) * P], wo_sb[:, j],
                                       start=j == 0, stop=j == PC - 1)
                mm.then_inc(o_done, 1)

            def turn_denominators():
                pe.wait_ge(den_done, CHUNKS)
                pe.wait_ge(nm_done, TILES * CHUNKS)
                for t in range(TILES):
                    mm = pe.transpose(ps_max[:, 0, t * P:(t + 1) * P],
                                      den_sb[:, (CHUNKS - 1) % 2, t * P:(t + 1) * P], con[:, IDENT:IDENT + P])
                mm.then_inc(dturn_done, 1)

            def spread_reciprocals(j):
                pe.wait_ge(rep_done[j], 1)
                pe.wait_ge(e_done, PAIRS * CHUNKS)
                for t in range(TILES):
                    mm = pe.matmul(ps_s[:, j, t * P:(t + 1) * P],
                                   rec[:, (CHUNKS - 1) % 2, j, t * P:(t + 1) * P],
                                   con[:, IDENT:IDENT + P], start=True, stop=True)
                mm.then_inc(spread_done, 1)

            project_queries(0, 0)
            project_keys()
            project_queries(0, 1)
            project_values()
            max_scores(0, 0)
            max_scores(0, 1)
            project_queries(1, 0)
            max_scores(0, 2)
            max_scores(0, 3)
            project_queries(1, 1)
            turn_max(0)
            for step in range(1, CHUNKS + 1):
                front, back = step, step - 1
                for slot in range(PAIRS):
                    k = PAIRS * back + slot
                    scores(back, slot)
                    if k >= 1 and slot != LATE_VALUES_SLOT:
                        values(k - 1)
                    if slot in out_slots(step) and step >= 3:
                        output(step - 3, out_slots(step).index(slot))
                    if slot in Q_SLOTS and front + 1 < CHUNKS:
                        project_queries(front + 1, Q_SLOTS.index(slot))
                    if slot == TURN_SLOT and front < CHUNKS:
                        turn_max(front)
                    if max_tiles(step, slot):
                        max_scores(*max_tiles(step, slot))
                    if slot == LATE_VALUES_SLOT:
                        values(k - 1)
            values(PAIRS * CHUNKS - 1)
            turn_denominators()
            output(CHUNKS - 2, 0)
            spread_reciprocals(0)
            spread_reciprocals(1)
            output(CHUNKS - 2, 1)
            output(CHUNKS - 1, 0)
            output(CHUNKS - 1, 1)

        @block.scalar
        def _(act):
            def high_x(c):
                act.wait_ge(in_xt[c % 2], 16 * (c // 2 + 1))
                if c >= 2:
                    act.wait_ge(q_done, 2 * (c - 1))
                act.activation(xt_h[:, c % 2], xt_sb[:, c % 2], ACT.Copy).then_inc(xh_done, 1)

            def high_queries(c, j):
                act.wait_ge(q_done, 2 * c + j + 1)
                if c >= NQ:
                    act.wait_ge(s_done, PAIRS * (c - NQ + 1))
                for half in range(2):
                    act.activation(q_high[rows(half), c % NQ, half, j], query_bank(2 * c + j)[rows(half), 0], ACT.Identity,
                                   bias=bcol[rows(half), j:j + 1]).then_inc(h_done, 1)

            def fixed_mask_rows(s):
                act.wait_ge(in_con, 32)
                for half in range(2):
                    other = rows(1 - half)
                    act.activation(keys_mask[other, s, half].rearrange("p j (h k) -> p (j h) k", k=KEYS),
                                   con[other, ID64:ID64 + KEYS].unsqueeze(1).to_broadcast([64, 8, KEYS]),
                                   ACT.Copy).then_inc(kfix_done, 1)

            def fixed_max_rows(s):
                for half in range(2):
                    other = rows(1 - half)
                    act.activation(keys_max[other, s, half].rearrange("p j (h k) -> p (j h) k", k=KEYS),
                                   con[other, ID64 + 8 * half:ID64 + 8 * half + 8].unsqueeze(2).to_broadcast([64, 8, KEYS]),
                                   ACT.Copy).then_inc(kfix_done, 1)

            def max_block(b, half):
                act.wait_ge(kblk_done, 2 * b + half + 1)
                if b >= 2:
                    act.wait_ge(s_done, PAIRS * PER_BATCH * (b - 1))
                act.activation(keys_max[rows(half), b % 2, half], keys_mask[rows(half), b % 2, half].bitcast(F32),
                               ACT.Copy).then_inc(kmax_done, 1)

            def exponentials(k):
                act.wait_ge(s_done, k + 1)
                if k >= NP_:
                    act.wait_ge(pv_done, k - NP_ + 1)
                act.activation(probs[:, k % NP_], ps_s[:, k % 2], ACT.Exp).then_inc(e_done, 1)

            def negative_max(c, half):
                act.wait_ge(turn_done, c + 1)
                if c in (0, 2):
                    act.wait_ge(fill_done, 2 if c == 0 else 4)
                if c >= NQ:
                    act.wait_ge(s_done, PAIRS * (c - NQ + 1))
                o = 64 * (1 - half)
                act.activation(q_low[o:o + HEADS, c % NQ, half],
                               turn_bank(c)[0:HEADS, 0].unsqueeze(1).to_broadcast([HEADS, 2, CHUNK]),
                               ACT.Copy).then_inc(neg_done, 1)

            def context_out(c, j):
                act.wait_ge(pv_done, PAIRS * c + 4 * j + 4)
                if c >= 2:
                    act.wait_ge(cn_done, 2 * (c - 1))
                act.activation(cx[:, c % 2, j], ps_c[:, 0], ACT.Copy).then_inc(cx_done, 1)

            def denominators_out(c):
                act.wait_ge(pv_done, PAIRS * (c + 1))
                if c >= 2:
                    act.wait_ge(den_in[c % 2], 16 * DEN_DMAS * (c // 2))
                act.activation(den_sb[:, c % 2], ps_d[:, 0], ACT.Copy).then_inc(den_done, 1)

            def normalised(c, t):
                act.wait_ge(ln_done, 4 * (c + 1) + (4 if c == CHUNKS - 1 and t >= 2 else 0))
                if c == CHUNKS - 1:
                    act.wait_ge(xl_done, CHUNKS)
                elif c >= 2:
                    act.wait_ge(stored[c % 2], 16 * (c // 2))
                act.activation(y_of(c)[:, t], res[:, c % 2, t], ACT.Identity, bias=shift[:, c % 2, t:t + 1],
                               scale=rstd[:, c % 2, t:t + 1]).then_inc(y_done, 1)

            act.wait_ge(in_wq, 16)
            act.activation(wq_h[:], wq_sb[:], ACT.Copy).then_inc(wqh_done, 1)
            high_x(0)
            high_x(1)
            high_queries(0, 0)
            act.wait_ge(kt_done, 2)
            act.activation(k_h[:], kt[:], ACT.Copy).then_inc(kh_done, 1)
            fixed_mask_rows(0)
            high_queries(0, 1)
            fixed_max_rows(0)
            max_block(0, 0)
            max_block(0, 1)
            high_queries(1, 0)
            high_queries(1, 1)
            high_x(2)
            negative_max(0, 0)
            for step in range(1, CHUNKS + 1):
                front, back = step, step - 1
                for slot in range(PAIRS):
                    exponentials(PAIRS * back + slot)
                    if step == 1 and slot == 0:
                        negative_max(0, 1)
                    if slot == 0 and back >= 1:
                        context_out(back - 1, 1)
                        denominators_out(back - 1)
                    if slot == 4:
                        context_out(back, 0)
                    if slot in Q_SLOTS and front + 1 < CHUNKS:
                        high_queries(front + 1, Q_SLOTS.index(slot))
                    if slot == X_HIGH_SLOT and front + 2 < CHUNKS:
                        high_x(front + 2)
                    if step == 1 and slot == 3:
                        fixed_mask_rows(1)
                    if slot - TURN_SLOT in (1, 2) and front < CHUNKS:
                        negative_max(front, slot - TURN_SLOT - 1)
                    if slot in KEY_COPY_SLOTS and next_batch(step):
                        max_block(next_batch(step), KEY_COPY_SLOTS.index(slot))
                    if step == 1 and slot == 5:
                        fixed_max_rows(1)
                    for t in range(TILES):
                        if (LAST_NORM_SLOTS if step == CHUNKS else NORM_SLOTS)[t] == slot and step >= 4:
                            normalised(step - 4, t)
                    for t in range(TILES):
                        if LATE_NORM_SLOTS[t] == slot and step == CHUNKS:
                            normalised(step - 3, t)
            context_out(CHUNKS - 1, 1)
            denominators_out(CHUNKS - 1)
            act.wait_ge(rq_done, 1)
            act.wait_ge(cn_done, 2 * (CHUNKS - 2))
            act.activation(*replicated(0), ACT.Copy).then_inc(rep_done[0], 1)
            for c in (CHUNKS - 2, CHUNKS - 1):
                for t in range(TILES):
                    normalised(c, t)

        @block.vector
        def _(dve):
            def low_x(c):
                dve.wait_ge(xh_done, c + 1)
                if c >= 2:
                    dve.wait_ge(q_done, 2 * (c - 1))
                dve.tensor_tensor(xt_l[:, c % 2], xt_sb[:, c % 2], xt_h[:, c % 2].bitcast(F32),
                                  ALU.subtract).then_inc(xl_done, 1)

            def mask_rows(c, half):
                dve.wait_ge(in_mask[c % 2], 16 * (c // 2 + 1))
                if c >= NQ:
                    dve.wait_ge(s_done, PAIRS * (c - NQ + 1))
                dve.tensor_scalar(q_high[rows(1 - half), c % NQ, half],
                                  m_sb[:, c % 2].unsqueeze(1).to_broadcast([KEYS, 2, CHUNK]),
                                  0.0, -BIG, ALU.is_equal, ALU.mult).then_inc(mask_done, 1)

            def low_queries(c, j):
                if c >= NQ:
                    dve.wait_ge(s_done, PAIRS * (c - NQ + 1))
                for half in range(2):
                    dve.wait_ge(h_done, 4 * c + 2 * j + half + 1)
                    dve.scalar_tensor_tensor(q_low[rows(half), c % NQ, half, j], query_bank(2 * c + j)[rows(half), 0],
                                             bcol[rows(half), j:j + 1],
                                             q_high[rows(half), c % NQ, half, j].bitcast(F32),
                                             ALU.add, ALU.subtract).then_inc(l_done, 1)

            def maxima(c, t):
                dve.wait_ge(max_done, TILES * c + t + 1)
                if c >= 2:
                    dve.wait_ge(turn_done, c - 1)
                dve.tensor_reduce(nmax[:, c % 2, t], max_bank(c, t)[:].rearrange("p a (h k) -> p (a h) k", k=KEYS),
                                  AX_X, ALU.max, negate=True).then_inc(nm_done, 1)

            def high_blocks(b, half):
                if b >= 2:
                    dve.wait_ge(s_done, PAIRS * PER_BATCH * (b - 1))
                r = rows(half)
                for j in range(2):
                    blk = dve.tensor_tensor(keys_mask[r, b % 2, half, j].rearrange("p (h k) -> p h k", k=KEYS),
                                            k_h[r, j, b].bitcast(F32).unsqueeze(1).to_broadcast([64, 4, KEYS]),
                                            con[r, BLOCK:BLOCK + 4].unsqueeze(2).to_broadcast([64, 4, KEYS]),
                                            ALU.mult)
                blk.then_inc(kblk_done, 1)

            def reciprocals(c):
                dve.wait_ge(den_in[c % 2], 16 * DEN_DMAS * (c // 2 + 1))
                if c >= 2:
                    dve.wait_ge(rec_in[c % 2], 16 * REC_DMAS * (c // 2))
                dve.reciprocal(rec_t[:, c % 2], den_t[:, c % 2]).then_inc(rec_done, 1)

            def divide(c):
                dve.wait_ge(rec_in[c % 2], 16 * REC_DMAS * (c // 2 + 1))
                dve.wait_ge(cx_done, 2 * (c + 1))
                if c >= 2:
                    dve.wait_ge(o_done, 2 * (c - 1))
                for j in range(2):
                    dve.tensor_tensor(cn[:, c % 2, j], cx[:, c % 2, j], rec[:, c % 2, j],
                                      ALU.mult).then_inc(cn_done, 1)

            def last_reciprocals():
                dve.wait_ge(dturn_done, 1)
                dve.reciprocal(rec_q[:].rearrange("p t (q r) -> p t q r", q=4),
                               ps_max[:, 0].rearrange("p (t q r) -> p t q r", t=TILES, q=4)[:, :, :, 0:4]
                               ).then_inc(rq_done, 1)
                dve.wait_ge(rq_done, 1)
                dve.tensor_copy(*replicated(1)).then_inc(rep_done[1], 1)

            def last_divide():
                c = CHUNKS - 1
                dve.wait_ge(cx_done, 2 * (c + 1))
                dve.wait_ge(o_done, 2 * (c - 1))
                for j in range(2):
                    dve.wait_ge(spread_done, j + 1)
                    dve.tensor_tensor(cn[:, c % 2, j], cx[:, c % 2, j], ps_s[:, j], ALU.mult).then_inc(cn_done, 1)

            def last_affine(c, i):
                n = 2 * (c - CHUNKS + 2) + i
                two = slice(2 * i, 2 * i + 2)
                dve.wait_ge(y_done, TILES * c + 2 * i + 2)
                dve.tensor_tensor(y_of(c)[:, two], y_of(c)[:, two], brow[:, 2].unsqueeze(1).to_broadcast([P, 2, D]),
                                  ALU.mult).then_inc(last_gam_done, 1)
                dve.wait_ge(last_gam_done, n)
                dve.tensor_tensor(y_of(c)[:, two], y_of(c)[:, two], brow[:, 3].unsqueeze(1).to_broadcast([P, 2, D]),
                                  ALU.add).then_inc(last_bet_done, 1)

            def residual(c, i):
                dve.wait_ge(o_done, 2 * c + i + 1)
                dve.wait_ge(xb_done, c + 1)
                if c >= 2:
                    dve.wait_ge(y_done, TILES * (c - 1))
                two = slice(2 * i, 2 * i + 2)
                dve.tensor_tensor(res[:, c % 2, two], out_tile(c, i).rearrange("p (t d) -> p t d", t=2),
                                  xb[:, c % 3, two], ALU.add).then_inc(res_done, 1)

            def moments(c, i):
                n = 2 * c + i + 1
                dve.wait_ge(res_done, n)
                if c >= 2:
                    dve.wait_ge(ln_done, 4 * (c - 1))
                for t in (2 * i, 2 * i + 1):
                    dve.bn_stats(stat[:, c % 2, t], res[:, c % 2, t]).then_inc(bn_done, 1)
                dve.wait_ge(bn_done, 2 * n)
                for t in (2 * i, 2 * i + 1):
                    dve.bn_aggr(mv[:, c % 2, t], stat[:, c % 2, t]).then_inc(mv_done, 1)

            dve.wait_ge(wqh_done, 1)
            dve.tensor_tensor(wq_l[:], wq_sb[:], wq_h[:].bitcast(F32), ALU.subtract).then_inc(wql_done, 1)
            low_x(0)
            mask_rows(0, 0)
            mask_rows(0, 1)
            low_x(1)
            dve.wait_ge(in_con, 32)
            dve.wait_ge(k_done, 1)
            for j in range(2):
                dve.tensor_scalar(kt[:, j], ps_max[:, j, 0:256].rearrange("p (b k) -> p b k", k=KEYS),
                                  bcol[:, 2 + j:3 + j], SCALE, ALU.add, ALU.mult).then_inc(kt_done, 1)
            mask_rows(1, 0)
            dve.wait_ge(fill_done, 2)
            dve.wait_ge(kh_done, 1)
            high_blocks(0, 0)
            high_blocks(0, 1)
            low_queries(0, 0)
            mask_rows(1, 1)
            maxima(0, 0)
            maxima(0, 1)
            dve.wait_ge(v_done, 1)
            dve.wait_ge(fill_done, 3)
            dve.wait_ge(in_rows, 16)
            for b in (0, 2):
                for h in range(2):
                    r, e = rows(h), slice(16 * h, 16 * h + 16)
                    dve.tensor_tensor(
                        v_bd[r, b:b + 2, :, e],
                        value_bank(b)[r, 0].rearrange("k (b p e) -> k b p e", b=2, e=32)[:, :, :, e],
                        brow[r, 0].rearrange("k (p e) -> k p e", e=32)[:, :, e].unsqueeze(1)
                        .to_broadcast([64, 2, PAIRS, 16]), ALU.add).then_inc(vbd_done, 1)
            maxima(0, 2)
            maxima(0, 3)
            low_queries(0, 1)
            low_queries(1, 0)
            low_queries(1, 1)
            low_x(2)
            dve.wait_ge(fill_done, 4)
            for step in range(1, CHUNKS + 1):
                front = step
                for slot in range(PAIRS):
                    if slot == out_slots(step)[0] and step >= 3:
                        residual(step - 3, 0)
                        moments(step - 3, 0)
                    if slot in KEY_SLOTS and next_batch(step):
                        high_blocks(next_batch(step), KEY_SLOTS.index(slot))
                    if slot in MASK_SLOTS and front + 1 < CHUNKS:
                        mask_rows(front + 1, MASK_SLOTS.index(slot))
                    if slot == RECIPROCAL_SLOT and step >= 2:
                        reciprocals(step - 2)
                    if slot == DIVIDE_SLOT and step >= 2:
                        divide(step - 2)
                    if max_tiles(step, slot):
                        maxima(*max_tiles(step, slot))
                    if slot in Q_SLOTS and front + 1 < CHUNKS:
                        low_queries(front + 1, Q_SLOTS.index(slot))
                    if slot == X_LOW_SLOT and front + 2 < CHUNKS:
                        low_x(front + 2)
                    if slot == out_slots(step)[1] and step >= 3:
                        residual(step - 3, 1)
                        moments(step - 3, 1)
            c = CHUNKS - 2
            last_reciprocals()
            residual(c, 0)
            last_divide()
            moments(c, 0)
            residual(c, 1)
            moments(c, 1)
            residual(c + 1, 0)
            moments(c + 1, 0)
            residual(c + 1, 1)
            moments(c + 1, 1)
            last_affine(c, 1)
            last_affine(c + 1, 0)
            last_affine(c + 1, 1)

        @block.gpsimd
        def _(pool):
            def with_bias(c):
                pool.wait_ge(in_x[c % 3], 16 * (c // 3 + 1))
                if c >= 3:
                    pool.wait_ge(res_done, 2 * (c - 2))
                pool.tensor_tensor(xb[:, c % 3], x_sb[:, c % 3],
                                   brow[:, 1].unsqueeze(1).to_broadcast([P, TILES, D]), ALU.add).then_inc(xb_done, 1)

            def low_blocks(b):
                if b >= 2:
                    pool.wait_ge(s_done, PAIRS * PER_BATCH * (b - 1))
                for j in range(2):
                    pool.tensor_tensor(
                        keys_low[:, b % 2, :, j].rearrange("p f (h k) -> p f h k", k=KEYS),
                        k_l[:, j, b].bitcast(F32).unsqueeze(1).unsqueeze(1).to_broadcast([P, 2, 4, KEYS]),
                        con[:, HEAD:HEAD + 8].rearrange("p (f h) -> p f h", f=2).unsqueeze(3)
                        .to_broadcast([P, 2, 4, KEYS]), ALU.mult).then_inc(klow_done, 1)

            def deviations(c, tiles=slice(0, TILES), n=None):
                i = c % 2
                n = 4 * c if n is None else n
                pool.wait_ge(mv_done, TILES * c + tiles.stop)
                if c >= 2:
                    pool.wait_ge(y_done, TILES * (c - 1))
                pool.tensor_scalar(veps[:, i, tiles], mv[:, i, tiles, 1], EPS, 1.0, ALU.add, ALU.mult).then_inc(ln_done, 1)
                pool.tensor_scalar(nmean[:, i, tiles], mv[:, i, tiles, 0], -1.0, 0.0, ALU.mult, ALU.add).then_inc(ln_done, 1)
                pool.wait_ge(ln_done, n + 2)
                pool.tensor_tensor(rstd[:, i, tiles], veps[:, i, tiles], half_neg[:, tiles], ALU.pow).then_inc(ln_done, 1)
                pool.wait_ge(ln_done, n + 3)
                pool.tensor_tensor(shift[:, i, tiles], nmean[:, i, tiles], rstd[:, i, tiles], ALU.mult).then_inc(ln_done, 1)

            def affine(c, i):
                two = slice(2 * i, 2 * i + 2)
                pool.wait_ge(y_done, TILES * c + 2 * i + 2)
                pool.tensor_tensor(y[:, c % 2, two], y[:, c % 2, two], brow[:, 2].unsqueeze(1).to_broadcast([P, 2, D]),
                                   ALU.mult).then_inc(gam_done, 1)
                pool.wait_ge(gam_done, 2 * c + i + 1)
                pool.tensor_tensor(y[:, c % 2, two], y[:, c % 2, two], brow[:, 3].unsqueeze(1).to_broadcast([P, 2, D]),
                                   ALU.add).then_inc(bet_done, 1)

            pool.memset(half_neg[:], -0.5).then_inc(fill_done, 1)
            pool.memset(q_low[:, 0:2].bitcast(F32), 0.0).then_inc(fill_done, 1)
            pool.memset(v_bd[:], 0.0).then_inc(fill_done, 1)
            pool.memset(q_low[:, 2:NQ].bitcast(F32), 0.0).then_inc(fill_done, 1)
            pool.wait_ge(fill_done, 4)
            pool.wait_ge(kt_done, 2)
            pool.wait_ge(kh_done, 1)
            pool.tensor_tensor(k_l[:], kt[:], k_h[:].bitcast(F32), ALU.subtract).then_inc(kl_done, 1)
            pool.wait_ge(kl_done, 1)
            pool.wait_ge(in_con, 32)
            low_blocks(0)
            pool.wait_ge(in_rows, 16)
            for step in range(1, CHUNKS + 1):
                if next_batch(step):
                    low_blocks(next_batch(step))
                with_bias(step - 1)
                if step == CHUNKS:
                    deviations(step - 3)
                if step >= 4:
                    affine(step - 4, 0)
                    affine(step - 4, 1)
                if 3 <= step < CHUNKS:
                    deviations(step - 3)
            c = CHUNKS - 3
            affine(c, 0)
            affine(c, 1)
            deviations(c + 1)
            deviations(c + 2, slice(0, 2))
            deviations(c + 2, slice(2, 4), 4 * (c + 2) + 4)
            affine(c + 1, 0)


def kernel(x, ctx_1024, mask_BxSxS2_ik1, L0_xattn_w_q, L0_xattn_b_q, L0_xattn_w_k, L0_xattn_b_k, L0_xattn_w_v,
           L0_xattn_b_v, L0_xattn_w_o, L0_xattn_b_o, L0_xattn_ln_gamma, L0_xattn_ln_beta):
    import concourse.bacc as bacc
    from concourse.bass_utils import run_bass_kernel_spmd

    x, ctx, mask = (np.asarray(a) for a in (x, ctx_1024, mask_BxSxS2_ik1))

    def weight(w):
        return np.ascontiguousarray(np.asarray(w).T.reshape(PC, P, D).transpose(1, 0, 2))

    chunks = x.reshape(CHUNKS, CHUNK, D)
    consts = np.zeros((P, CONSTS), np.float32)
    row = np.arange(P)
    consts[row, IDENT + row] = 1
    consts[row, ID64 + row % 64] = 1
    consts[row, HEAD + row // DK] = 1
    consts[row, BLOCK + row % 64 // DK] = 1
    for j in range(2):
        consts[row, ONES + 32 * j + 2 * (row // 64) + j] = 1
    arrays = {
        "xT": np.ascontiguousarray(chunks.transpose(0, 2, 1).reshape(CHUNKS, PC, P, CHUNK).transpose(0, 2, 1, 3)),
        "x": np.ascontiguousarray(chunks.reshape(CHUNKS, TILES, P, D).transpose(0, 2, 1, 3)),
        "maskT": np.ascontiguousarray(mask.reshape(CHUNKS, CHUNK, KEYS).transpose(0, 2, 1)),
        "ctxT": np.ascontiguousarray(np.broadcast_to(
            ctx.transpose(2, 0, 1).reshape(PC, P, BATCHES, 1, KEYS), (PC, P, BATCHES, 2, KEYS)
        ).transpose(1, 0, 2, 3, 4)),
        "wq": weight(L0_xattn_w_q), "wk": weight(L0_xattn_w_k),
        "wv": weight(L0_xattn_w_v), "wo": weight(L0_xattn_w_o),
        "bias_cols": np.ascontiguousarray(np.concatenate(
            [np.asarray(b).reshape(PC, P).T for b in (L0_xattn_b_q, L0_xattn_b_k)], axis=1)),
        "bias_rows": np.stack([np.asarray(b) for b in (
            L0_xattn_b_v, L0_xattn_b_o, L0_xattn_ln_gamma, L0_xattn_ln_beta)])[None],
        "consts": consts,
    }
    nc = bacc.Bacc("TRN2", target_bir_lowering=False, num_devices=1)
    args = [nc.dram_tensor(n, a.shape, mybir.dt.from_np(a.dtype), kind="ExternalInput").ap()
            for n, a in arrays.items()]
    out = nc.dram_tensor("out", (CHUNKS, P, TILES, D), F32, kind="ExternalOutput").ap()
    build(nc, *args, out)
    r = run_bass_kernel_spmd(nc, [arrays], core_ids=[0])
    return r.results[0]["out"].transpose(0, 2, 1, 3).reshape(BATCHES, QUERIES, D)
```
